# Optimizing a Trainium2 kernel written in Bass

```python
import numpy as np
import jax
import jax.numpy as jnp

def _softmax(x, axis=-1):
    return jax.nn.softmax(x, axis=axis)

def _gelu(x):
    return jax.nn.gelu(x, approximate=True)

def _silu(x):
    return jax.nn.silu(x)

def _sigmoid(x):
    return jax.nn.sigmoid(x)

def _layernorm(x, axis=-1, eps=1e-05):
    m = jnp.mean(x, axis=axis, keepdims=True)
    v = jnp.var(x, axis=axis, keepdims=True)
    return (x - m) / jnp.sqrt(v + eps)

def _scatter_add(tgt, idx, src, axis=0):
    return tgt.at[idx].add(src)

def _segment_sum(src, seg, n):
    return jax.ops.segment_sum(src, seg, n)
kernel_name = 'mk_perceiver_d1_seqx_r2_6412f3'

def setup_inputs(seed: int=0):
    np.random.seed(seed)
    _w = jnp.asarray

    def _rec_inputs():
        import jax
        import jax.numpy as jnp
        _rk = jax.random.key(seed)
        x = 7.22e-05 + 1 * jax.random.normal(jax.random.fold_in(_rk, 1), (1, 512, 1024), jnp.float32)
        _lenS = 512 - jax.random.randint(jax.random.fold_in(_rk, 7), (1,), 0, max(1, 512 // 4) + 1, jnp.int32)
        _lenS2 = 8192 - jax.random.randint(jax.random.fold_in(_rk, 8), (1,), 0, max(1, 8192 // 4) + 1, jnp.int32)
        _ctx_512P = jax.random.normal(jax.random.fold_in(_rk, 11), (1, 16, 256), jnp.float32)
        _ctx_512c = jax.random.dirichlet(jax.random.fold_in(_rk, 511), 0.3 * jnp.ones((16,), jnp.float32), (1, 8192))
        _ctx_512t = jnp.einsum('bsk,bkd->bsd', _ctx_512c, _ctx_512P)
        _ctx_512t = _ctx_512t * jax.lax.rsqrt(jnp.mean(jnp.square(_ctx_512t)) + 1e-12) * 0.953939
        ctx_512 = -0.000514642 + 1.00011 * (_ctx_512t + 0.3 * jax.random.normal(jax.random.fold_in(_rk, 611), (1, 8192, 256), jnp.float32))
        return (x, ctx_512)
    x, ctx_512 = _rec_inputs()

    def _L0_xattn_setup():
        import jax, jax.numpy as jnp
        import numpy as np
        B, S, H, NH, L = (2, 1024, 1024, 16, 256)
        HD = H // NH
        key = jax.random.key(seed)
        k1, k2, k3, k4, k5 = jax.random.split(key, 5)
        scale = 0.02
        return {'q': jax.random.normal(k1, (B, S, H), dtype=jnp.float32), 'latent_kv': jax.random.normal(k2, (B, S, L), dtype=jnp.float32), 'Wq': jax.random.normal(k3, (H, H), dtype=jnp.float32) * scale, 'Wkv_expand': jax.random.normal(k4, (2 * H, L), dtype=jnp.float32) * scale, 'Wout': jax.random.normal(k5, (H, H), dtype=jnp.float32) * scale}
    _L0_xattn_all = _L0_xattn_setup()
    _L0_xattn_in = {k: v for k, v in _L0_xattn_all.items() if k in ('Wq', 'Wkv_expand', 'Wout')}
    del _L0_xattn_all

    def _L0_attn_setup():
        import jax, jax.numpy as jnp
        import numpy as np
        EPS_NORM = 1e-08
        EPS_Q = 1e-05

        def rms_norm(x, w):
            var = jnp.mean(x * x, axis=-1, keepdims=True)
            return x * jax.lax.rsqrt(var + EPS_NORM) * w

        def activation_quant(x):
            scale = 127.0 / jnp.clip(jnp.max(jnp.abs(x), axis=-1, keepdims=True), EPS_Q, None)
            return jnp.clip(jnp.round(x * scale), -128, 127) / scale

        def weight_quant(w):
            scale = 1.0 / jnp.clip(jnp.mean(jnp.abs(w)), EPS_Q, None)
            return jnp.clip(jnp.round(w * scale), -1, 1) / scale

        def bitlinear(x, w, norm_w):
            xn = rms_norm(x, norm_w)
            xq = xn + jax.lax.stop_gradient(activation_quant(xn) - xn)
            wq = w + jax.lax.stop_gradient(weight_quant(w) - w)
            return jnp.einsum('bsh,oh->bso', xq, wq)
        key = jax.random.key(seed)
        k1, k2, k3 = jax.random.split(key, 3)
        H, I = (1024, 2816)
        x = jax.random.normal(k1, (4, 1024, H), dtype=jnp.float32)
        w_gate = jax.random.normal(k2, (2 * I, H), dtype=jnp.float32) * (1.0 / np.sqrt(H))
        w_down = jax.random.normal(k3, (H, I), dtype=jnp.float32) * (1.0 / np.sqrt(I))
        norm_gate = jnp.ones((H,), dtype=jnp.float32)
        norm_down = jnp.ones((I,), dtype=jnp.float32)
        return {'x': x, 'w_gate': w_gate, 'norm_gate': norm_gate, 'w_down': w_down, 'norm_down': norm_down}
    _L0_attn_all = _L0_attn_setup()
    _L0_attn_in = {k: v for k, v in _L0_attn_all.items() if k in ('w_gate', 'norm_gate', 'w_down', 'norm_down')}
    del _L0_attn_all

    def _L0_ffn_setup():
        import jax, jax.numpy as jnp
        import numpy as np
        B, S, D = (4, 1024, 1024)
        E, F, K = (8, 512, 2)
        SF = 512
        EPS = 1e-06

        def _rmsnorm(x, w, eps=EPS):
            var = jnp.mean(x * x, axis=-1, keepdims=True)
            return x * jax.lax.rsqrt(var + eps) * w
        key = jax.random.key(seed)
        ks = jax.random.split(key, 9)
        g = lambda k, shape, scale: jax.random.normal(k, shape, jnp.float32) * scale
        return {'x': g(ks[0], (B, S, D), 1.0), 'rms_weight': jnp.ones((D,), jnp.float32), 'router_w': g(ks[1], (D, E), 0.02), 'w_gate': g(ks[2], (E, D, F), 0.02), 'w_up': g(ks[3], (E, D, F), 0.02), 'w_down': g(ks[4], (E, F, D), 0.02), 'sw_gate': g(ks[5], (D, SF), 0.02), 'sw_up': g(ks[6], (D, SF), 0.02), 'sw_down': g(ks[7], (SF, D), 0.02)}
    _L0_ffn_all = _L0_ffn_setup()
    _L0_ffn_in = {k: v for k, v in _L0_ffn_all.items() if k in ('rms_weight', 'router_w', 'w_gate', 'w_up', 'w_down', 'sw_gate', 'sw_up', 'sw_down')}
    del _L0_ffn_all
    return {'x': x, 'ctx_512': ctx_512, 'L0_xattn_Wq': _L0_xattn_in['Wq'], 'L0_xattn_Wkv_expand': _L0_xattn_in['Wkv_expand'], 'L0_xattn_Wout': _L0_xattn_in['Wout'], 'L0_attn_w_gate': _L0_attn_in['w_gate'], 'L0_attn_norm_gate': _L0_attn_in['norm_gate'], 'L0_attn_w_down': _L0_attn_in['w_down'], 'L0_attn_norm_down': _L0_attn_in['norm_down'], 'L0_ffn_rms_weight': _L0_ffn_in['rms_weight'], 'L0_ffn_router_w': _L0_ffn_in['router_w'], 'L0_ffn_w_gate': _L0_ffn_in['w_gate'], 'L0_ffn_w_up': _L0_ffn_in['w_up'], 'L0_ffn_w_down': _L0_ffn_in['w_down'], 'L0_ffn_sw_gate': _L0_ffn_in['sw_gate'], 'L0_ffn_sw_up': _L0_ffn_in['sw_up'], 'L0_ffn_sw_down': _L0_ffn_in['sw_down']}

def reference(x, ctx_512, L0_xattn_Wq, L0_xattn_Wkv_expand, L0_xattn_Wout, L0_attn_w_gate, L0_attn_norm_gate, L0_attn_w_down, L0_attn_norm_down, L0_ffn_rms_weight, L0_ffn_router_w, L0_ffn_w_gate, L0_ffn_w_up, L0_ffn_w_down, L0_ffn_sw_gate, L0_ffn_sw_up, L0_ffn_sw_down):
    import jax
    import jax.numpy as jnp

    def _L0_xattn_ref(q, latent_kv, Wq, Wkv_expand, Wout):
        import jax, jax.numpy as jnp
        import numpy as np
        B, S, H, NH, L = (2, 1024, 1024, 16, 256)
        HD = H // NH
        b, sq, _ = q.shape
        sk = latent_kv.shape[1]
        qp = q @ Wq.T
        kv = latent_kv @ Wkv_expand.T
        k, v = jnp.split(kv, 2, axis=-1)
        qh = qp.reshape(b, sq, NH, HD).transpose(0, 2, 1, 3)
        kh = k.reshape(b, sk, NH, HD).transpose(0, 2, 1, 3)
        vh = v.reshape(b, sk, NH, HD).transpose(0, 2, 1, 3)
        inv_sqrt_d = 1.0 / jnp.sqrt(jnp.float32(HD))
        scores = jnp.einsum('bhqd,bhkd->bhqk', qh, kh) * inv_sqrt_d
        causal = jnp.tril(jnp.ones((sq, sk), dtype=bool))
        scores = jnp.where(causal, scores, jnp.finfo(scores.dtype).min)
        attn = jax.nn.softmax(scores, axis=-1)
        out = jnp.einsum('bhqk,bhkd->bhqd', attn, vh)
        out = out.transpose(0, 2, 1, 3).reshape(b, sq, H)
        return out @ Wout.T

    def _L0_attn_ref(x, w_gate, norm_gate, w_down, norm_down):
        import jax, jax.numpy as jnp
        import numpy as np
        EPS_NORM = 1e-08
        EPS_Q = 1e-05

        def rms_norm(x, w):
            var = jnp.mean(x * x, axis=-1, keepdims=True)
            return x * jax.lax.rsqrt(var + EPS_NORM) * w

        def activation_quant(x):
            scale = 127.0 / jnp.clip(jnp.max(jnp.abs(x), axis=-1, keepdims=True), EPS_Q, None)
            return jnp.clip(jnp.round(x * scale), -128, 127) / scale

        def weight_quant(w):
            scale = 1.0 / jnp.clip(jnp.mean(jnp.abs(w)), EPS_Q, None)
            return jnp.clip(jnp.round(w * scale), -1, 1) / scale

        def bitlinear(x, w, norm_w):
            xn = rms_norm(x, norm_w)
            xq = xn + jax.lax.stop_gradient(activation_quant(xn) - xn)
            wq = w + jax.lax.stop_gradient(weight_quant(w) - w)
            return jnp.einsum('bsh,oh->bso', xq, wq)
        y = bitlinear(x, w_gate, norm_gate)
        gate, up = jnp.split(y, 2, axis=-1)
        h = gate * jax.nn.sigmoid(gate) * up
        return bitlinear(h, w_down, norm_down)

    def _L0_ffn_ref(x, rms_weight, router_w, w_gate, w_up, w_down, sw_gate, sw_up, sw_down):
        import jax, jax.numpy as jnp
        import numpy as np
        B, S, D = (4, 1024, 1024)
        E, F, K = (8, 512, 2)
        SF = 512
        EPS = 1e-06

        def _rmsnorm(x, w, eps=EPS):
            var = jnp.mean(x * x, axis=-1, keepdims=True)
            return x * jax.lax.rsqrt(var + eps) * w
        b, s, d = x.shape
        e = router_w.shape[1]
        h = _rmsnorm(x, rms_weight)
        ht = h.reshape(-1, d)
        t = ht.shape[0]
        logits = ht @ router_w
        probs = jax.nn.softmax(logits, axis=-1)
        topv, topi = jax.lax.top_k(probs, K)
        topv = topv / jnp.sum(topv, axis=-1, keepdims=True)
        w_dense = jnp.zeros((t, e), ht.dtype).at[jnp.arange(t)[:, None], topi].set(topv)
        g = jnp.einsum('td,edf->tef', ht, w_gate)
        u = jnp.einsum('td,edf->tef', ht, w_up)
        eo = jnp.einsum('tef,efd->ted', jax.nn.silu(g) * u, w_down)
        moe = jnp.einsum('te,ted->td', w_dense, eo)
        sh = jax.nn.silu(ht @ sw_gate) * (ht @ sw_up) @ sw_down
        return (moe + sh).reshape(b, s, d)
    x = x + _L0_xattn_ref(_layernorm(x, axis=-1), ctx_512, L0_xattn_Wq, L0_xattn_Wkv_expand, L0_xattn_Wout)
    x = x + _L0_attn_ref(_layernorm(x, axis=-1), L0_attn_w_gate, L0_attn_norm_gate, L0_attn_w_down, L0_attn_norm_down)
    x = x + _L0_ffn_ref(_layernorm(x, axis=-1), L0_ffn_rms_weight, L0_ffn_router_w, L0_ffn_w_gate, L0_ffn_w_up, L0_ffn_w_down, L0_ffn_sw_gate, L0_ffn_sw_up, L0_ffn_sw_down)
    return x

_drawn_inputs = setup_inputs


def setup_inputs(seed=0):
    import zlib

    import numpy as np

    out = dict(_drawn_inputs(seed))
    spreads = {'L0_attn_norm_gate': (1.0, 0.2),
     'L0_attn_norm_down': (1.0, 0.2),
     'L0_ffn_rms_weight': (1.0, 0.2)}
    factors = {}
    for name, (base, spread) in spreads.items():
        noise = np.random.default_rng([zlib.crc32(name.encode()), seed]).standard_normal(out[name].shape)
        drawn = base * np.exp(spread * noise) if base else spread * noise
        out[name] = jnp.asarray(drawn.astype(out[name].dtype))
    for name, factor in factors.items():
        out[name] = (out[name] * factor).astype(out[name].dtype)
    return out
```

```python
from contextlib import ExitStack

import concourse.bass as bass
from concourse import mybir

P = 128
TOK, DM, LAT = 512, 1024, 256
NT = TOK // P
KD = DM // P
KL = LAT // P
NH, HD = 16, 64
NPAIR = NH // 2
FB, KB = 2816, 22
GC, GW = 11, 256
NE, FE, KE = 8, 512, 4
NGRP = NE + 1
RAW = 2048
NABS = 2 * GC + GC
ABSP = 4
MAXT = NT + (2 * TOK // P + NE - 1)
XT_TILES = MAXT + 2
GATHER = (XT_TILES + 1) * P
DRAM_TILES = MAXT + NT + 2
VB = (6, 7, 0, 1)
WO_SLOTS = (0, 2, 3, 4)
HGRP = ((0, 8), (8, 16), (16, 22))
MAGIC = 12582912.0
HBLK = [(3, 0), (2, 512), (0, 896), (1, 1024)]
SOFF = dict(HBLK)
TBLK = [(0, 0), (1, 512), (3, 896), (2, 1024)]
TOFF = dict(TBLK)
STRIP = 1280

f32, f32r, bf16 = mybir.dt.float32, mybir.dt.float32r, mybir.dt.bfloat16
i32, u32 = mybir.dt.int32, mybir.dt.uint32
ALU, ACT, AX = mybir.AluOpType, mybir.ActivationFunctionType, mybir.AxisListType


def program(nc, x, ctxT, wv, wqk, wo, wbit, n_gate, n_down, n_rms, wrt, wmoe, out, rows_dram):
    es = ExitStack()
    with es:
        sem_names = []

        def sem(name):
            sem_names.append(name)
            return es.enter_context(nc.semaphore(name))

        base = (nc.sbuf_base + 63) // 64 * 64

        class Region:
            def __init__(self, at):
                self.at = at

            def __call__(self, name, shape, dt):
                n = 2 if dt == bf16 else 4
                for s in shape[1:]:
                    n *= s
                t = nc.alloc_sbuf_tensor_at(name, shape, dt, offset=self.at)
                self.at += (n + 31) // 32 * 32
                assert self.at <= nc.sbuf_usable_end, (name, self.at)
                return t

        keep = Region(base)
        XRES = keep("XRES", [P, NT, DM], f32)
        IDF = keep("IDF", [P, P], f32)
        IDB = keep("IDB", [P, P], bf16)
        MASK = keep("MASK", [P, P], bf16)
        TRI = keep("TRI", [P, P], bf16)
        ONEB = keep("ONEB", [P, P], bf16)
        ONEF = keep("ONEF", [P, P], f32)
        CST = keep("CST", [P, 4], f32)
        BN = keep("BN", [P, NT, 2, 6], f32)
        MV = keep("MV", [P, NT, 2], f32)
        SM = keep("SM", [P, 128], f32)
        ACCW = keep("ACCW", [P, NABS], f32)
        IOTA8 = keep("IOTA8", [P, 8], f32)
        CNT = keep("CNT", [1, 32], i32)
        SLOT = keep("SLOT", [P, 2, NT], i32)
        RT = keep("RT", [P, 512], f32)
        M0B = keep("M0B", [P, 2, NT, 8], bf16)
        MSB = keep("MSB", [P, NT, 8], bf16)
        I8 = keep("I8", [P, NT, 8], u32)
        NM = RT[:, 0:8].rearrange("p (a b) -> p a b", a=2)
        RS = RT[:, 8:16].rearrange("p (a b) -> p a b", a=2)
        RSI = RT[:, 16:24].rearrange("p (a b) -> p a b", a=2)
        WS = RT[:, 24:26]
        MC = RT[:, 26:28]
        SW = RT[:, 28:30]
        E1 = RT[:, 32:36].rearrange("p (a b) -> p a b", b=1)
        WT = RT[:, 36:48].rearrange("p (a b) -> p a b", b=NT)
        LG = RT[:, 64:96].rearrange("p (a b) -> p a b", b=8)
        M8 = RT[:, 96:128].rearrange("p (a b) -> p a b", b=8)
        I8F = RT[:, 128:160].rearrange("p (a b) -> p a b", b=8)
        CTF = RT[:, 160:192]
        NEF = RT[:, 192:200]
        AT = RT[:, 200:232].rearrange("p (a b) -> p a b", b=8)
        SLM = RT[:, 232:296].rearrange("p (k t e) -> p k t e", k=2, t=NT)
        SLF = RT[:, 296:304]
        start = keep.at

        a = Region(start)
        XTH = a("XTH", [P, KD, TOK], f32r)
        XTL = a("XTL", [P, KD, TOK], f32r)
        CTH = a("CTH", [P, KL, TOK], f32r)
        CTL = a("CTL", [P, KL, TOK], f32r)
        OTH = a("OTH", [P, KD, TOK], f32r)
        OTL = a("OTL", [P, KD, TOK], f32r)
        WQH = a("WQH", [P, KD + KL, P], f32r)
        WQL = a("WQL", [P, KD + KL, P], f32r)
        QH = a("QH", [P, TOK], f32r)
        QL = a("QL", [P, TOK], f32r)
        KH = a("KH", [P, TOK], f32r)
        KLo = a("KLo", [P, TOK], f32r)
        VH = a("VH", [P, NT, P], f32r)
        VL = a("VL", [P, NT, P], f32r)
        PTH = [a(f"PTH{h}", [P, STRIP], f32r) for h in range(2)]
        PTL = [a(f"PTL{h}", [P, STRIP], f32r) for h in range(2)]
        V = a("V", [P, NT, DM], f32)
        PR = [a(f"PR{h}", [P, STRIP], f32) for h in range(2)]
        RA = [a(f"RA{j}", [P, RAW], f32) for j in range(5)]
        ZERO = a("ZERO", [P, DM], f32)
        CTX = nc.alloc_sbuf_tensor_at("CTX", [P, KL, TOK], f32, offset=V.manual_sbuf_range[0])
        WVH = nc.alloc_sbuf_tensor_at("WVH", [P, KL, DM], f32r, offset=OTH.manual_sbuf_range[0])
        WVL = nc.alloc_sbuf_tensor_at("WVL", [P, KL, DM], f32r, offset=OTL.manual_sbuf_range[0])
        XN = [nc.alloc_sbuf_tensor_at(f"XN{h}", [P, DM], f32, offset=PR[h].manual_sbuf_range[0]) for h in range(2)]
        w = Region(XTH.manual_sbuf_range[0])
        WOH = [w(f"WOH{s}", [P, 2, DM], f32r) for s in range(2)]
        WOL = [w(f"WOL{s}", [P, 2, DM], f32r) for s in range(2)]

        b = Region(start)
        XQ = b("XQ", [P, KD, TOK], bf16)
        TG = [b(f"TG{s}", [P, KD, 2 * GW], bf16) for s in range(2)]
        TD = b("TD", [P, KB, DM], bf16)
        HB = b("HB", [P, NT, FB], f32)
        HQ = b("HQ", [P, FB], bf16)
        HQT = [b(f"HQT{s}", [P, KB, P], bf16) for s in range(2)]
        SG = b("SG", [P, NT, GW], f32)
        NG = b("NG", [P, DM], f32)
        ND = b("ND", [P, FB], f32)
        RB = [b(f"RB{j}", [P, RAW], f32) for j in range(4)]
        JB = nc.alloc_sbuf_tensor_at("JB", [P, FB], bf16, offset=TG[0].manual_sbuf_range[0])
        z = Region(HB.manual_sbuf_range[0])
        Z = z("Z", [P, NT, DM], f32)
        ZQ = [z(f"ZQ{s}", [P, DM], bf16) for s in range(2)]
        ZJ = z("ZJ", [P, DM], f32)

        c = Region(start)
        WH = [c(f"WH{m}", [P, RAW * 2], f32r) for m in range(3)]
        WL = [c(f"WL{m}", [P, RAW * 2], f32r) for m in range(3)]
        ETH = c("ETH", [P, KD, P], f32r)
        ETL = c("ETL", [P, KD, P], f32r)
        HTH = c("HTH", [P, KE, P], f32r)
        HTL = c("HTL", [P, KE, P], f32r)
        SI = c("SI", [P, FE], f32)
        HE = c("HE", [P, FE], f32)
        XG = c("XG", [P, DM], f32)
        YS = c("YS", [P, DM], f32)
        c("SPARE", [P, 2, DM], f32)
        RC = [c(f"RC{j}", [P, RAW], f32) for j in range(6)]
        H3 = nc.alloc_sbuf_tensor_at("H3", [P, NT, DM], f32, offset=XG.manual_sbuf_range[0])
        JC = nc.alloc_sbuf_tensor_at("JC", [P, DM], f32, offset=SI.manual_sbuf_range[0])
        r = Region(RC[2].manual_sbuf_range[0])
        H3T = r("H3T", [P, KD, P], f32)
        WR = r("WR", [P, KD, 8], f32)
        NR = r("NR", [P, DM], f32)
        g = Region(WH[0].manual_sbuf_range[0])
        GA = g("GA", [P, NT, DM], f32)
        GB = g("GB", [P, NT, DM], f32)
        GS = g("GS", [P, NT, DM], f32)

        BK = [es.enter_context(nc.psum_tensor(f"BK{i}", [P, 1536 if i in (0, 3) else 512], f32))
              for i in (0, 3, 6, 7)]
        STR = BK[0:2]
        bank = [BK[i // 3][:, i % 3 * 512:i % 3 * 512 + 512] if i < 6 else BK[i - 4][:, :] for i in range(8)]

        S = {}

        def s(name):
            if name not in S:
                S[name] = sem(name)
            return S[name]

        for n in ("const", "bn", "mv", "v_eps", "sqrt", "newton", "ln",
                  "x_in0", "x_in1", "x_in2", "x_in3", "ctx_in", "norm_in",
                  "xn", "xt_pe", "xt_hi", "xt_lo", "ct_hi", "ct_lo", "wv_hi", "wv_lo", "v_pe", "v_ev0", "v_ev1",
                  "wq_hi", "wq_lo", "q_pe", "k_pe", "q_hi", "q_lo", "k_hi", "k_lo", "vp_hi", "vp_lo", "s_pe",
                  "nmax", "exp", "rsum", "pn", "t_pe", "pt_hi", "pt_lo", "av_pe", "ot_hi", "ot_lo", "bank67",
                  "absa", "absd", "wo_hi", "wo_lo", "y_pe", "x2",
                  "wsum", "wsum_pe", "wscale", "z_sq", "z", "zq", "zt_pe", "xq",
                  "rnd", "tern1", "tern", "g_pe", "silu", "h", "h_sq", "hz", "hq", "ht_pe", "hqt", "d_pe", "x3",
                  "h3", "h3t_pe", "h3t", "lg_pe", "top", "e1", "pos_pe", "cnt", "slots", "scat", "zero_in", "zero",
                  "shared_st", "dself", "aself",
                  "slots_m", "zn", "rows", "y_all", "m_hi", "m_lo", "e_in", "et_pe", "et_hi", "et_lo", "gate_pe", "up_pe", "esilu", "eh", "ht2_pe",
                  "ht_hi", "ht_lo", "y2_pe", "ys_a", "ys_d", "y_st", "fin_in0", "fin_in1", "fin_in2", "fin_in3", "fin", "out"):
            s(n)
        in_a = [sem(f"raw_a{j}") for j in range(5)]
        free_a = [sem(f"free_a{j}") for j in range(5)]
        in_b = [sem(f"raw_b{j}") for j in range(4)]
        free_b = [sem(f"free_b{j}") for j in range(4)]
        in_c = [sem(f"raw_c{j}") for j in range(6)]
        free_c = [sem(f"free_c{j}") for j in range(6)]

        blk = es.enter_context(nc.Block())

        def r3(ap, n):
            return ap.rearrange("p (a b) -> p a b", a=n)

        def three(e, dst, pairs, first, last):
            m, n = None, len(pairs)
            for i, (sh, sl, mh, ml) in enumerate(pairs):
                for j, (st, mv) in enumerate(((sh, mh), (sh, ml), (sl, mh))):
                    m = e.matmul(dst, st, mv, start=first and i == 0 and j == 0, stop=last and i == n - 1 and j == 2)
            return m

        def highs(e, dst, pairs):
            for i, (sh, mh, ml) in enumerate(pairs):
                e.matmul(dst, sh, mh, start=i == 0, stop=False)
                e.matmul(dst, sh, ml, start=False, stop=False)

        def lows(e, dst, pairs):
            for i, (sl, mh) in enumerate(pairs):
                m = e.matmul(dst, sl, mh, start=False, stop=i == len(pairs) - 1)
            return m

        class Own:
            def __init__(self, e, name):
                self.e, self.sem, self.n = e, s(name), 0

            def __call__(self, ins):
                ins.then_inc(self.sem, 1)
                self.n += 1
                self.e.wait_ge(self.sem, self.n)

        own = {}

        def col(k):
            return SM[:, 4 * k:4 * k + 4]

        def inv_sqrt(e, v, q, dst, sync_value):
            o = own["dve"]
            e.wait_ge(s("sqrt"), sync_value)
            t = col(14)[:, 0:v.shape[1]]
            o(e.reciprocal(dst, q))
            o(e.tensor_tensor(t, dst, dst, ALU.mult))
            o(e.tensor_tensor(t, t, v, ALU.mult))
            o(e.tensor_scalar(t, t, -0.5, 1.5, ALU.mult, ALU.add))
            o(e.tensor_tensor(dst, dst, t, ALU.mult))

        def group_of(e, gi):
            e_n = CNT[0:1, bass.ds(gi, 1)] if not isinstance(gi, int) else CNT[0:1, gi:gi + 1]
            e_t = CNT[0:1, bass.ds(gi + 10, 1)] if not isinstance(gi, int) else CNT[0:1, gi + 10:gi + 11]
            return e.value_load(e_n, min_val=1, max_val=NT), e.value_load(e_t, min_val=0, max_val=MAXT - 1)

        def waits(e, *pairs):
            at = [(s(n) if isinstance(n, str) else n, v if isinstance(v, int) else e.snap(v)) for n, v in pairs]
            for sm, v in at:
                e.wait_ge(sm, v)

        roots = [0]

        def root(e, v, q):
            roots[0] += 1
            e.wait_ge(s("v_eps"), roots[0])
            e.activation(q, v, ACT.Sqrt).then_inc(s("sqrt"), 1)

        veps = [0]

        def layer_norm_stats(e):
            o = own["dve"]
            for t in range(NT):
                if veps[0] == 0:
                    e.wait_ge(s(f"x_in{t}"), 16)
                for h in range(2):
                    ins = e.bn_stats(BN[:, t, h, :], XRES[:, t, h * 512:h * 512 + 512])
                o(ins)
                o(e.bn_aggr(MV[:, t, :], BN[:, t, :, :].rearrange("p a b -> p (a b)")))
            e.tensor_scalar(col(2), MV[:, :, 1:2].rearrange("p a b -> p (a b)"), 1e-5, None, ALU.add)\
                .then_inc(s("v_eps"), 1)
            veps[0] += 1
            e.wait_ge(s("v_eps"), veps[0])
            inv_sqrt(e, col(2), col(3), col(0), veps[0])
            e.scalar_tensor_tensor(out=col(1), in0=MV[:, :, 0:1].rearrange("p a b -> p (a b)"), scalar=-1.0,
                                   in1=col(0), op0=ALU.mult, op1=ALU.mult).then_inc(s("ln"), 1)

        @blk.sync
        def _(e):
            e.dma_start(XRES[:, 0, :], x[0:P, :]).then_inc(s("x_in0"), 16)
            for t in range(1, NT):
                e.dma_start(XRES[:, t, :], x[t * P:t * P + P, :]).then_inc(s(f"x_in{t}"), 16)
            e.dma_start(CTX[:, :, :], ctxT).then_inc(s("ctx_in"), 16)
            e.dma_start(RA[0][:, :], wv).then_inc(in_a[0], 16)

            def qk_load(c):
                e.wait_ge(free_a[0], c + 1)
                src = wqk[c] if isinstance(c, int) else wqk[bass.ds(c, 1), :, :].rearrange("a p n -> p (a n)")
                e.dma_start(RA[0][:, 0:STRIP], src).then_inc(in_a[0], 16)

            def sum_loads(c, first):
                for j in range(1, 5):
                    if not first:
                        e.wait_ge(free_a[j], c)
                    e.dma_start(RA[j][:, :], wbit[bass.ds(c * ABSP + j - 1, 1), :, :]
                                .rearrange("a p n -> p (a n)")).then_inc(in_a[j], 16)
            qk_load(0)
            sum_loads(0, True)
            qk_load(1)
            with e.Fori(1, NPAIR - 1) as c:
                qk_load(c + 1)
                sum_loads(c, False)
            sum_loads(NPAIR - 1, False)
            e.wait_ge(free_a[1], NPAIR)
            e.dma_start(RA[1][:, :], wbit[NABS - 1]).then_inc(in_a[1], 16)
            for m, j in enumerate((0, 2, 3, 4)):
                e.wait_ge(free_a[j], NPAIR + 1 if j == 0 else NPAIR)
                e.dma_start(RA[j][:, :], wo[m]).then_inc(in_a[j], 16)

            e.wait_ge(s("wo_lo"), 4)
            e.wait_ge(s("y_pe"), 4)
            e.wait_ge(free_a[1], NPAIR + 1)
            e.dma_start(NG[:, :], n_gate.partition_broadcast(P)).then_inc(s("norm_in"), 16)
            e.dma_start(ND[:, :], n_down.partition_broadcast(P)).then_inc(s("norm_in"), 16)

            def bit_load(j, chunk, waits):
                if waits is not None:
                    e.wait_ge(free_b[j], waits)
                src = wbit[chunk] if isinstance(chunk, int) else \
                    wbit[bass.ds(chunk, 1), :, :].rearrange("a p n -> p (a n)")
                e.dma_start(RB[j][:, :], src).then_inc(in_b[j], 16)
            for j in range(4):
                bit_load(j, j, None)
            with e.Fori(1, 8) as k:
                for j in range(4):
                    bit_load(j, k * 4 + j, k)
            bit_load(0, NABS - 1, 8)

            e.wait_ge(s("x3"), NT)
            e.dma_start(NR[:, :], n_rms.partition_broadcast(P)).then_inc(s("norm_in"), 16)
            e.dma_start(WR[:, :, :], wrt).then_inc(s("norm_in"), 16)
            e.wait_ge(s("h3"), NT)
            for t in range(NT):
                e.dma_start(rows_dram[(t + 1) * P:(t + 2) * P, :], H3[:, t, :]).then_inc(s("shared_st"), 16)

            def group_loads(gi, first):
                for j in range(6):
                    if first:
                        if j == 2:
                            e.wait_ge(s("lg_pe"), NT)
                            e.wait_ge(s("h3"), NT)
                    else:
                        e.wait_ge(free_c[j], gi)
                    e.dma_start(RC[j][:, :], wmoe[bass.ds(gi * 6 + j, 1), :, :].rearrange("a p n -> p (a n)"))\
                        .then_inc(in_c[j], 16)
            group_loads(0, True)
            e.wait_ge(s("rows"), 1)
            e.dma_start(XG[:, :], rows_dram[P:2 * P, :]).then_inc(s("e_in"), 16)
            e.wait_ge(s("et_pe"), 2)
            e.dma_start(XG[:, :], rows_dram[2 * P:3 * P, :]).then_inc(s("e_in"), 16)
            e.sem_inc(s("y_st"), 16)

            def tile(t):
                row, row2 = e.snap(t * P), e.snap(t * P + 3 * P)
                waits(e, ("ys_a", t + 1), ("ys_d", t + 1), ("y_st", t * 16 + 16))
                e.dma_start(rows_dram[bass.ds(row, P), :], YS[:, :]).then_inc(s("y_st"), 16)
                e.wait_ge(s("et_pe"), t * 2 + 4)
                e.dma_start(XG[:, :], rows_dram[bass.ds(row2, P), :]).then_inc(s("e_in"), 16)
            e.wait_ge(s("cnt"), 1)
            with e.Fori(0, NE) as gi:
                group_loads(gi + 1, False)
                n, t0 = group_of(e, gi)
                with e.Fori(0, n) as i:
                    tile(t0 + i)
            n, t0 = group_of(e, NE)
            with e.Fori(0, n) as i:
                tile(t0 + i)
            total = e.value_load(CNT[0:1, 31:32], min_val=NT + NE, max_val=MAXT)
            row = e.snap(total * P)
            waits(e, ("ys_a", total + 1), ("ys_d", total + 1), ("y_st", total * 16 + 16))
            e.dma_start(rows_dram[bass.ds(row, P), :], YS[:, :]).then_inc(s("y_st"), 16)
            waits(e, ("y_st", total * 16 + 32), ("e_in", total * 16 + 32))
            e.sem_inc(s("y_all"), 1)

            for t in range(NT):
                e.wait_ge(s("fin"), t + 1)
                e.dma_start(out[t * P:t * P + P, :], XRES[:, t, :]).then_inc(s("out"), 16)
            e.wait_ge(s("out"), 16 * NT)

        @blk.gpsimd
        def _(e):
            for ins in (e.memset(IDF[:, :], 0.0), e.memset(IDB[:, :], 0.0), e.memset(MASK[:, :], 0.0),
                        e.memset(TRI[:, :], 1.0), e.memset(ONEB[:, :], 1.0), e.memset(ONEF[:, :], 1.0),
                        e.memset(CST[:, :], MAGIC), e.memset(ZERO[:, :], 0.0),
                        e.iota(I8[:, 0, :], pattern=[[1, 8]], base=0, channel_multiplier=0)):
                ins.then_inc(s("const"), 1)
            e.wait_ge(s("const"), 9)
            for m in (IDF, IDB):
                e.affine_select(out=m[:, :], in_=m[:, :], compare_op=ALU.not_equal, fill=1.0, base=0,
                                pattern=[[-1, P]], channel_multiplier=1).then_inc(s("const"), 1)
            e.affine_select(out=MASK[:, :], in_=MASK[:, :], compare_op=ALU.is_ge, fill=-1e30, base=0,
                            pattern=[[-1, P]], channel_multiplier=1).then_inc(s("const"), 1)
            e.affine_select(out=TRI[:, :], in_=TRI[:, :], compare_op=ALU.is_gt, fill=0.0, base=0,
                            pattern=[[1, P]], channel_multiplier=-1).then_inc(s("const"), 1)
            e.tensor_copy(IOTA8[:, :], I8[:, 0, :]).then_inc(s("const"), 1)
            def w_lo(c):
                e.wait_ge(s("wq_hi"), c + 1)
                e.tensor_tensor(WQL[:, :, :].rearrange("p a b -> p (a b)"), RA[0][:, 0:STRIP],
                                WQH[:, :, :].rearrange("p a b -> p (a b)").bitcast(f32), ALU.subtract)\
                    .then_inc(free_a[0], 1)

            def v_lo(c):
                e.wait_ge(s("vp_hi"), c + 1)
                e.tensor_tensor(VL[:, :, :], V[:, :, bass.ds(c * P, P)], VH[:, :, :].bitcast(f32), ALU.subtract)\
                    .then_inc(s("vp_lo"), 1)
            w_lo(0)
            with e.Fori(1, NPAIR) as c:
                w_lo(c)
                v_lo(c - 1)
            v_lo(NPAIR - 1)
            for k in range(NT, XT_TILES):
                e.dma_start(rows_dram[(k + 1) * P:(k + 2) * P, :], ZERO[:, :]).then_inc(s("zero"), 16)

            e.wait_ge(s("slots"), 1)
            e.wait_ge(s("h3"), NT)
            e.wait_ge(s("zero"), 16 * (XT_TILES - NT))
            for k in range(2):
                for t in range(NT):
                    e.indirect_dma_start(rows_dram[0:GATHER, :], bass.IndirectOffsetOnAxis(ap=SLOT[:, k, t:t + 1], axis=0),
                                         H3[:, t, :], None).then_inc(s("scat"), 16)
            e.wait_ge(s("scat"), 16 * 2 * NT)
            e.wait_ge(s("shared_st"), 16 * NT)
            e.sem_inc(s("rows"), 1)
            e.wait_ge(s("y_all"), 1)
            for t in range(NT):
                e.dma_start(GS[:, t, :], rows_dram[(t + 1) * P:(t + 2) * P, :]).then_inc(s(f"fin_in{t}"), 16)
                for k, dst in enumerate((GA, GB)):
                    e.indirect_dma_start(dst[:, t, :], None, rows_dram[0:GATHER, :],
                                         bass.IndirectOffsetOnAxis(ap=SLOT[:, k, t:t + 1], axis=0))\
                        .then_inc(s(f"fin_in{t}"), 16)

        @blk.vector
        def _(e):
            own["dve"] = o = Own(e, "dself")
            e.sem_inc(s("ot_lo"), 1)
            e.sem_inc(s("h"), 8)
            layer_norm_stats(e)
            for n in range(2 * NT):
                t, q = divmod(n, 2)
                e.wait_ge(s("xt_hi"), n + 1)
                e.tensor_tensor(XTL[:, 4 * q:4 * q + 4, t * P:t * P + P], r3(bank[2 + n % 4], 4),
                                XTH[:, 4 * q:4 * q + 4, t * P:t * P + P].bitcast(f32), ALU.subtract)\
                    .then_inc(s("xt_lo"), 1)
            e.wait_ge(s("ct_hi"), 1)
            e.tensor_tensor(CTL[:, :, :], CTX[:, :, :], CTH[:, :, :].bitcast(f32), ALU.subtract)\
                .then_inc(s("ct_lo"), 1)
            e.wait_ge(s("wv_hi"), 1)
            e.tensor_tensor(WVL[:, :, :], r3(RA[0][:, :], 2), WVH[:, :, :].bitcast(f32), ALU.subtract)\
                .then_inc(free_a[0], 1)
            for t in range(NT):
                e.wait_ge(s("v_pe"), 2 * t + 2)
                e.tensor_copy(V[:, t, 512:1024], bank[VB[(2 * t + 1) % 4]]).then_inc(s("v_ev1"), 1)

            def absum(j, column, n):
                e.wait_ge(in_a[j], n)
                e.tensor_reduce(ACCW[:, column], RA[j][:, :], AX.X, ALU.add, apply_absolute_value=True)\
                    .then_inc(free_a[j], 1)

            def close_pair(c):
                for h in range(2):
                    e.wait_ge(s("pt_hi"), 2 * c - 1 + h)
                    e.tensor_tensor(PTL[h][:, :], STR[h][:, 0:STRIP], PTH[h][:, :].bitcast(f32), ALU.subtract)\
                        .then_inc(s("pt_lo"), 1)
                for h in range(2):
                    rows = slice(HD * h, HD * h + HD)
                    e.wait_ge(s("ot_hi"), 2 * c - 1 + h)
                    e.tensor_tensor(OTL[rows, bass.ds(c - 1, 1), :].rearrange("p a n -> p (a n)"),
                                    bank[6 + h][rows, :],
                                    OTH[rows, bass.ds(c - 1, 1), :].rearrange("p a n -> p (a n)").bitcast(f32),
                                    ALU.subtract).then_inc(s("ot_lo"), 1)

            def pair(c, first):
                e.wait_ge(s("q_hi"), c + 1)
                e.scalar_tensor_tensor(out=QL[:, :], in0=bank[6], scalar=HD ** -0.5, in1=QH[:, :].bitcast(f32),
                                       op0=ALU.mult, op1=ALU.subtract).then_inc(s("q_lo"), 1)
                e.wait_ge(s("k_hi"), c + 1)
                e.tensor_tensor(KLo[:, :], bank[7], KH[:, :].bitcast(f32), ALU.subtract).then_inc(s("k_lo"), 1)
                if not first:
                    close_pair(c)
                for h in range(2):
                    e.wait_ge(s("s_pe"), 2 * c + h + 1)
                    for i, off in HBLK:
                        ins = e.tensor_reduce(NM[:, h, i:i + 1], STR[h][:, off:off + P * (i + 1)], AX.X, ALU.max,
                                              negate=True)
                    ins.then_inc(s("nmax"), 1)
                absum(2, bass.ds(c * ABSP + 1, 1), c * 16 + 16)
                for h in range(2):
                    e.wait_ge(s("exp"), 2 * c + h + 1)
                    e.reciprocal(RSI[:, h, :], RS[:, h, :]).then_inc(s("rsum"), 1)
                    e.wait_ge(s("rsum"), 2 * c + h + 1)
                    for i, off in HBLK:
                        v = PR[h][:, off:off + P * (i + 1)]
                        ins = e.tensor_scalar(v, v, RSI[:, h, i:i + 1], None, ALU.mult)
                    ins.then_inc(s("pn"), 1)
                absum(4, bass.ds(c * ABSP + 3, 1), c * 16 + 16)
            pair(0, True)
            with e.Fori(1, NPAIR) as c:
                pair(c, False)
            close_pair(NPAIR)

            for m, j in enumerate(WO_SLOTS):
                e.wait_ge(s("wo_hi"), m + 1)
                e.tensor_tensor(WOL[m % 2][:, :, :], r3(RA[j][:, :], 2), WOH[m % 2][:, :, :].bitcast(f32),
                                ALU.subtract).then_inc(s("wo_lo"), 1)
            e.wait_ge(s("y_pe"), 4)
            for n in range(8):
                v = XRES[:, n // 2, n % 2 * 512:n % 2 * 512 + 512]
                e.tensor_tensor(v, bank[n], v, ALU.add).then_inc(s("x2"), 1)
            for j in (2, 4):
                e.wait_ge(free_a[j], NPAIR)
            e.wait_ge(free_a[1], NPAIR + 1)
            e.wait_ge(free_a[3], NPAIR)
            e.tensor_reduce(WS[:, 0:1], ACCW[:, 0:2 * GC], AX.X, ALU.add)
            e.tensor_reduce(WS[:, 1:2], ACCW[:, 2 * GC:NABS], AX.X, ALU.add).then_inc(s("wsum"), 1)
            e.wait_ge(s("wsum_pe"), 1)
            o(e.tensor_scalar(MC[:, 0:1], bank[0][:, 0:1], 1.0 / (2 * FB * DM), 1e-5, ALU.mult, ALU.max))
            o(e.tensor_scalar(MC[:, 1:2], bank[0][:, 1:2], 1.0 / (FB * DM), 1e-5, ALU.mult, ALU.max))
            e.reciprocal(SW[:, :], MC[:, :]).then_inc(s("wscale"), 1)
            e.wait_ge(s("x2"), 8)
            layer_norm_stats(e)

            def rms_weighted(T, NW, eps, done):
                e.wait_ge(s("z_sq"), done)
                e.tensor_scalar(col(4), col(15), 1.0 / DM, eps, ALU.mult, ALU.add).then_inc(s("v_eps"), 1)
                veps[0] += 1
                e.wait_ge(s("v_eps"), veps[0])
                inv_sqrt(e, col(4), col(3), col(5), veps[0])
                for t in range(NT):
                    yield e.scalar_tensor_tensor(out=T[:, t, :], in0=T[:, t, :], scalar=col(5)[:, t:t + 1],
                                                 in1=NW[:, :], op0=ALU.mult, op1=ALU.mult)
            e.wait_ge(s("norm_in"), 32)
            for ins in rms_weighted(Z, NG, 1e-8, NT):
                o(ins)
            for t in range(NT):
                ins = e.tensor_reduce(col(6)[:, t:t + 1], Z[:, t, :], AX.X, ALU.max, apply_absolute_value=True)
            o(ins)
            o(e.tensor_scalar(col(7), col(6), 1e-5, None, ALU.max))
            o(e.reciprocal(col(8), col(7)))
            o(e.tensor_scalar(col(8), col(8), 127.0, None, ALU.mult))
            e.tensor_scalar(col(9), col(7), MC[:, 0:1], 1.0 / 127.0, ALU.mult, ALU.mult).then_inc(s("z"), 1)
            for t in range(NT):
                o(e.tensor_scalar(Z[:, t, :], Z[:, t, :], col(8)[:, t:t + 1], MAGIC, ALU.mult, ALU.add))
                if t >= 2:
                    e.wait_ge(s("zt_pe"), t - 1)
                e.tensor_scalar(ZQ[t % 2][:, :], Z[:, t, :], -MAGIC, None, ALU.add).then_inc(s("zq"), 1)

            def ternary(dst, j, n, use):
                e.wait_ge(s("rnd"), n + 1)
                e.tensor_scalar(dst, RB[j][:, :], -MAGIC, 1.0, ALU.add, ALU.min).then_inc(free_b[j], 1)
                e.wait_ge(free_b[j], use)
                e.tensor_scalar(dst, dst, -1.0, None, ALU.max).then_inc(s("tern"), 1)

            def gate_weights(p, j0, n, use):
                for q in range(2):
                    ternary(TG[p][:, 4 * q:4 * q + 4, :].rearrange("p a b -> p (a b)"), j0 + q, n + q, use)

            def gate_group(c, p):
                for t in range(NT):
                    e.wait_ge(s("silu"), 4 * c + t + 1)
                    e.scalar_tensor_tensor(out=HB[:, t, bass.ds(c * GW, GW)], in0=bank[4 * p + t][:, GW:2 * GW],
                                           scalar=col(9)[:, t:t + 1], in1=SG[:, t, :],
                                           op0=ALU.mult, op1=ALU.mult).then_inc(s("h"), 1)
            gate_weights(0, 0, 0, 1)
            with e.Fori(0, GC // 2) as it:
                waits(e, ("g_pe", it * 8 + 1), ("rnd", it * 4 + 3))
                gate_weights(1, 2, it * 4 + 2, it + 1)
                gate_group(it * 2, 0)
                waits(e, ("g_pe", it * 8 + 5), ("rnd", it * 4 + 5))
                gate_weights(0, 0, it * 4 + 4, it + 2)
                gate_group(it * 2 + 1, 1)
            gate_group(GC - 1, 0)

            def hidden_quant(t):
                one = slice(t, t + 1)
                e.wait_ge(s("h_sq"), t + 1)
                e.tensor_scalar(col(4)[:, one], col(10)[:, one], 1.0 / FB, 1e-8, ALU.mult, ALU.add)\
                    .then_inc(s("v_eps"), 1)
                veps[0] += 1
                o(e.tensor_tensor(HB[:, t, :], HB[:, t, :], ND[:, :], ALU.mult))
                o(e.tensor_reduce(col(11)[:, one], HB[:, t, :], AX.X, ALU.max, apply_absolute_value=True))
                e.wait_ge(s("v_eps"), veps[0])
                inv_sqrt(e, col(4)[:, one], col(3)[:, one], col(12)[:, one], veps[0])
                o(e.tensor_scalar(col(13)[:, one], col(11)[:, one], col(12)[:, one], 1e-5, ALU.mult, ALU.max))
                o(e.reciprocal(col(6)[:, one], col(13)[:, one]))
                o(e.tensor_scalar(col(6)[:, one], col(6)[:, one], col(12)[:, one], 127.0, ALU.mult, ALU.mult))
                e.tensor_scalar(col(8)[:, one], col(13)[:, one], MC[:, 1:2], 1.0 / 127.0, ALU.mult, ALU.mult)
                o(e.tensor_scalar(HB[:, t, :], HB[:, t, :], col(6)[:, one], MAGIC, ALU.mult, ALU.add))
                if t:
                    e.wait_ge(s("ht_pe"), 3 * t)
                e.tensor_scalar(HQ[:, :], HB[:, t, :], -MAGIC, None, ALU.add).then_inc(s("hq"), 1)

            def down_weights(i0, i1):
                for i in range(i0, i1):
                    n = 2 * GC + i
                    ternary(TD[:, 2 * i:2 * i + 2, :].rearrange("p a b -> p (a b)"), n % 4, n, n // 4 + 1)

            def second_residual(t):
                for q in range(2):
                    v = XRES[:, t, q * 512:q * 512 + 512]
                    e.wait_ge(s("d_pe"), 2 * t + q + 1)
                    ins = e.scalar_tensor_tensor(out=v, in0=bank[2 * (t % 2) + q], scalar=col(8)[:, t:t + 1], in1=v,
                                                 op0=ALU.mult, op1=ALU.add)
                ins.then_inc(s("x3"), 1)
            e.wait_ge(s("h"), 8 + 4 * GC)
            hidden_quant(0)
            down_weights(0, 6)
            hidden_quant(1)
            down_weights(6, GC)
            hidden_quant(2)
            second_residual(0)
            hidden_quant(3)
            for t in range(1, NT):
                second_residual(t)

            e.wait_ge(s("x3"), NT)
            layer_norm_stats(e)
            e.wait_ge(s("norm_in"), 64)
            for ins in rms_weighted(H3, NR, 1e-6, 2 * NT):
                ins.then_inc(s("h3"), 1)
            for t in range(NT):
                e.wait_ge(s("h3t_pe"), 2 * t + 2)
                if t:
                    e.wait_ge(s("lg_pe"), t)
                e.tensor_copy(H3T[:, 4:8, :], r3(bank[2 * (t % 2) + 1], 4)).then_inc(s("h3t"), 1)
            e.wait_ge(s("lg_pe"), NT)
            o(e.tensor_copy(LG[:, :, :], bank[4][:, 0:32].rearrange("p (a b) -> p a b", a=NT)))
            for t in range(NT):
                ins = e.max(M8[:, t, :], LG[:, t, :])
            o(ins)
            for t in range(NT):
                ins = e.max_index(I8[:, t, :], M8[:, t, :], LG[:, t, :])
            o(ins)
            o(e.tensor_copy(I8F[:, :, :], I8[:, :, :]))
            e.tensor_tensor(E1[:, :, :], M8[:, :, 1:2], M8[:, :, 0:1], ALU.subtract).then_inc(s("top"), 1)
            for k in range(2):
                for t in range(NT):
                    ins = e.tensor_scalar(M0B[:, k, t, :], IOTA8[:, :], I8F[:, t, k:k + 1], None, ALU.is_equal)
            o(ins)
            e.tensor_tensor(MSB[:, :, :], M0B[:, 0, :, :], M0B[:, 1, :, :], ALU.add).then_inc(s("slots_m"), 1)
            e.wait_ge(s("pos_pe"), 1)
            n_e = bank[5][:, 32:40]
            o(e.memset(CTF[:, :], 0.0))
            o(e.memset(CTF[:, 0:1], float(NT)))
            o(e.memset(CTF[:, 11:12], float(NT)))
            o(e.tensor_copy(NEF[:, :], n_e))
            o(e.tensor_scalar(CTF[:, 1:9], NEF[:, :], float(P), 1.0, ALU.is_gt, ALU.add))
            for k in (2, 3):
                o(e.scalar_tensor_tensor(out=CTF[:, 1:9], in0=NEF[:, :], scalar=float(k * P), in1=CTF[:, 1:9],
                                         op0=ALU.is_gt, op1=ALU.add))
            for k in range(1, NE):
                o(e.tensor_tensor(CTF[:, 11 + k:12 + k], CTF[:, 10 + k:11 + k], CTF[:, k:k + 1], ALU.add))
            o(e.tensor_tensor(CTF[:, 31:32], CTF[:, 18:19], CTF[:, 8:9], ALU.add))
            e.tensor_copy(CNT[:, :], CTF[0:1, :]).then_inc(s("cnt"), 1)
            for t in range(NT):
                ins = e.scalar_tensor_tensor(out=AT[:, t, :], in0=CTF[:, 11:19], scalar=float(P),
                                             in1=bank[5][:, 8 * t:8 * t + 8], op0=ALU.mult, op1=ALU.add)
            o(ins)
            for k in range(2):
                ins = e.tensor_tensor(SLM[:, k, :, :], AT[:, :, :], M0B[:, k, :, :], ALU.mult)
            o(ins)
            o(e.tensor_reduce(SLF[:, :], SLM[:, :, :, :].rearrange("p k t e -> p (k t) e"), AX.X, ALU.add))
            e.tensor_scalar(SLOT[:, :, :].rearrange("p a b -> p (a b)"), SLF[:, :], float(P), None, ALU.add)\
                .then_inc(s("slots"), 1)
            e.wait_ge(s("e1"), 1)
            o(e.tensor_scalar(WT[:, 2, :], WT[:, 1, :], 1.0, None, ALU.add))
            o(e.reciprocal(WT[:, 0, :], WT[:, 2, :]))
            o(e.tensor_tensor(WT[:, 1, :], WT[:, 1, :], WT[:, 0, :], ALU.mult))

            def split(gi):
                for j in range(6):
                    m, q = divmod(j, 2)
                    e.wait_ge(s("m_hi"), gi * 6 + j + 1)
                    e.tensor_tensor(WL[m][:, q * RAW:q * RAW + RAW], RC[j][:, :],
                                    WH[m][:, q * RAW:q * RAW + RAW].bitcast(f32), ALU.subtract)\
                        .then_inc(free_c[j], 1)

            def rows_lo(t):
                for q in range(2):
                    e.wait_ge(s("et_hi"), t * 2 + q + 1)
                    e.tensor_tensor(ETL[:, 4 * q:4 * q + 4, :], r3(bank[4 + q], 4),
                                    ETH[:, 4 * q:4 * q + 4, :].bitcast(f32), ALU.subtract).then_inc(s("et_lo"), 1)

            def result(t):
                waits(e, ("y2_pe", t + 1), ("y_st", t * 16 + 16))
                e.tensor_copy(YS[:, 512:1024], bank[3]).then_inc(s("ys_d"), 1)

            def tile(t):
                result(t)
                waits(e, ("esilu", t + 1), ("up_pe", t + 1))
                e.tensor_tensor(HE[:, :], bank[1], SI[:, :], ALU.mult).then_inc(s("eh"), 1)
                e.wait_ge(s("ht_hi"), t + 1)
                e.tensor_tensor(HTL[:, :, :], r3(bank[6], 4), HTH[:, :, :].bitcast(f32), ALU.subtract)\
                    .then_inc(s("ht_lo"), 1)
                rows_lo(t + 1)
            e.wait_ge(s("cnt"), 1)
            e.wait_ge(s("scat"), 16 * 2 * NT)
            e.wait_ge(s("shared_st"), 16 * NT)
            rows_lo(0)
            split(0)
            with e.Fori(0, NE) as gi:
                n, t0 = group_of(e, gi)
                with e.Fori(0, n) as i:
                    tile(t0 + i)
                split(gi + 1)
            n, t0 = group_of(e, NE)
            with e.Fori(0, n) as i:
                tile(t0 + i)
            total = e.value_load(CNT[0:1, 31:32], min_val=NT + NE, max_val=MAXT)
            result(total)
            for t in range(NT):
                v = XRES[:, t, :]
                e.wait_ge(s(f"fin_in{t}"), 16 * 3)
                o(e.tensor_tensor(v, v, GS[:, t, :], ALU.add))
                o(e.scalar_tensor_tensor(out=v, in0=GA[:, t, :], scalar=WT[:, 0, t:t + 1], in1=v,
                                         op0=ALU.mult, op1=ALU.add))
                e.scalar_tensor_tensor(out=v, in0=GB[:, t, :], scalar=WT[:, 1, t:t + 1], in1=v,
                                       op0=ALU.mult, op1=ALU.add).then_inc(s("fin"), 1)

        @blk.scalar
        def _(e):
            def normed(dst, t, name):
                e.activation(dst, XRES[:, t, :], ACT.Identity, bias=col(1)[:, t:t + 1], scale=col(0)[:, t:t + 1])\
                    .then_inc(s(name), 1)

            root(e, col(2), col(3))
            e.wait_ge(s("ln"), 1)

            def xt_evac(t):
                for q in range(2):
                    n = 2 * t + q
                    e.wait_ge(s("xt_pe"), n + 1)
                    e.activation(XTH[:, 4 * q:4 * q + 4, t * P:t * P + P], r3(bank[2 + n % 4], 4), ACT.Copy)\
                        .then_inc(s("xt_hi"), 1)
            for t in range(NT):
                if t >= 2:
                    e.wait_ge(s("xt_pe"), 2 * (t - 1))
                normed(XN[t % 2][:, :], t, "xn")
                if t:
                    xt_evac(t - 1)
            e.wait_ge(s("ctx_in"), 16)
            e.activation(CTH[:, :, :], CTX[:, :, :], ACT.Copy).then_inc(s("ct_hi"), 1)
            e.wait_ge(in_a[0], 16)
            e.activation(WVH[:, :, :], r3(RA[0][:, :], 2), ACT.Copy).then_inc(s("wv_hi"), 1)
            xt_evac(NT - 1)

            def w_hi(c):
                e.wait_ge(in_a[0], c * 16 + 32)
                e.activation(WQH[:, :, :].rearrange("p a b -> p (a b)"), RA[0][:, 0:STRIP], ACT.Copy)\
                    .then_inc(s("wq_hi"), 1)
            w_hi(0)
            for t in range(NT):
                e.wait_ge(s("v_pe"), 2 * t + 1)
                e.activation(V[:, t, 0:512], bank[VB[2 * t % 4]], ACT.Copy).then_inc(s("v_ev0"), 1)

            def absum(j, column, n):
                e.wait_ge(in_a[j], n)
                e.activation(RA[j][:, :], RA[j][:, :], ACT.Abs, accum_out=ACCW[:, column]).then_inc(free_a[j], 1)

            def close_probs(c):
                for h in range(2):
                    e.wait_ge(s("t_pe"), 2 * c - 1 + h)
                    e.activation(PTH[h][:, :], STR[h][:, 0:STRIP], ACT.Copy).then_inc(s("pt_hi"), 1)

            def close_out(c):
                for h in range(2):
                    rows = slice(HD * h, HD * h + HD)
                    e.wait_ge(s("av_pe"), 2 * c - 1 + h)
                    e.activation(OTH[rows, bass.ds(c - 1, 1), :].rearrange("p a n -> p (a n)"), bank[6 + h][rows, :],
                                 ACT.Copy).then_inc(s("ot_hi"), 1)

            def pair(c, first, last):
                e.wait_ge(s("q_pe"), c + 1)
                e.activation(QH[:, :], bank[6], ACT.Copy, scale=HD ** -0.5).then_inc(s("q_hi"), 1)
                e.wait_ge(s("k_pe"), c + 1)
                e.activation(KH[:, :], bank[7], ACT.Copy).then_inc(s("k_hi"), 1)
                if not first:
                    close_probs(c)
                if not last:
                    w_hi(c + 1)
                if not first:
                    close_out(c)
                else:
                    e.wait_ge(s("v_ev1"), NT)
                    e.wait_ge(s("v_ev0"), NT)
                e.activation(VH[:, :, :], V[:, :, bass.ds(c * P, P)], ACT.Copy).then_inc(s("vp_hi"), 1)
                for h in range(2):
                    e.wait_ge(s("nmax"), 2 * c + h + 1)
                    for i, off in HBLK:
                        ins = e.activation(PR[h][:, off:off + P * (i + 1)], STR[h][:, off:off + P * (i + 1)],
                                           ACT.Exp, bias=NM[:, h, i:i + 1], accum_out=RS[:, h, i:i + 1])
                    ins.then_inc(s("exp"), 1)
                absum(1, bass.ds(c * ABSP, 1), c * 16 + 16)
                absum(3, bass.ds(c * ABSP + 2, 1), c * 16 + 16)
            pair(0, True, False)
            with e.Fori(1, NPAIR - 1) as c:
                pair(c, False, False)
            pair(NPAIR - 1, False, True)
            close_probs(NPAIR)
            close_out(NPAIR)
            absum(1, slice(NABS - 1, NABS), NPAIR * 16 + 16)
            for m, j in enumerate(WO_SLOTS):
                e.wait_ge(in_a[j], 16 * (NPAIR + 2 if j == 0 else NPAIR + 1))
                if m >= 2:
                    e.wait_ge(s("y_pe"), m - 1)
                e.activation(WOH[m % 2][:, :, :], r3(RA[j][:, :], 2), ACT.Copy).then_inc(s("wo_hi"), 1)

            root(e, col(2), col(3))
            e.wait_ge(s("ln"), 2)

            def squares(T, J, t, acc, count):
                e.activation(J, T, ACT.Square, accum_out=acc).then_inc(s(count), 1)
            for t in range(NT):
                normed(Z[:, t, :], t, "zn")
                e.wait_ge(s("zn"), t + 1)
                squares(Z[:, t, :], ZJ[:, :], t, col(15)[:, t:t + 1], "z_sq")
            root(e, col(4), col(3))

            def rounded(j, n, use, which):
                e.wait_ge(in_b[j], use * 16 if isinstance(use, int) else use * 16)
                e.activation(RB[j][:, :], RB[j][:, :], ACT.Identity, bias=CST[:, 0:1], scale=SW[:, which:which + 1])\
                    .then_inc(s("rnd"), 1)
            e.wait_ge(s("wscale"), 1)
            for j in range(2):
                rounded(j, j, 1, 0)
            for t in range(NT):
                e.wait_ge(s("zt_pe"), t + 1)
                e.activation(XQ[:, :, t * P:t * P + P], r3(bank[4 + t].bitcast(bf16), 8), ACT.Copy)\
                    .then_inc(s("xq"), 1)
            e.wait_ge(s("z"), 1)

            def gate_group(c, p):
                for t in range(NT):
                    waits(e, ("g_pe", 4 * c + t + 2), ("h", 4 * c + t + 5))
                    e.activation(SG[:, t, :], bank[4 * p + t][:, 0:GW], ACT.Silu, scale=col(9)[:, t:t + 1])\
                        .then_inc(s("silu"), 1)
            with e.Fori(0, GC // 2) as it:
                for j in (2, 3):
                    rounded(j, None, it + 1, 0)
                gate_group(it * 2, 0)
                for j in (0, 1):
                    rounded(j, None, it + 2, 0)
                gate_group(it * 2 + 1, 1)
            gate_group(GC - 1, 0)

            def hidden_squares(t):
                squares(HB[:, t, :], JB[:, :], t, col(10)[:, t:t + 1], "h_sq")
                root(e, col(4)[:, t:t + 1], col(3)[:, t:t + 1])

            def down_round(i0, i1):
                for i in range(i0, i1):
                    n = 2 * GC + i
                    rounded(n % 4, n, n // 4 + 1, 1)

            def hidden_t(t):
                for q, (k0, k1) in enumerate(HGRP):
                    e.wait_ge(s("ht_pe"), 3 * t + q + 1)
                    e.activation(HQT[t % 2][:, k0:k1, :], r3(bank[4 + q].bitcast(bf16)[:, 0:P * (k1 - k0)], k1 - k0),
                                 ACT.Copy).then_inc(s("hqt"), 1)
            e.wait_ge(s("h"), 8 + 4 * GC)
            hidden_squares(0)
            down_round(0, 6)
            hidden_squares(1)
            down_round(6, GC)
            hidden_t(0)
            hidden_squares(2)
            hidden_t(1)
            hidden_squares(3)
            hidden_t(2)
            hidden_t(3)

            root(e, col(2), col(3))
            e.wait_ge(s("ln"), 3)
            for t in range(NT):
                normed(H3[:, t, :], t, "zn")
                e.wait_ge(s("zn"), NT + t + 1)
                squares(H3[:, t, :], JC[:, :], t, col(15)[:, t:t + 1], "z_sq")
            root(e, col(4), col(3))
            for t in range(NT):
                e.wait_ge(s("h3t_pe"), 2 * t + 1)
                if t:
                    e.wait_ge(s("lg_pe"), t)
                e.activation(H3T[:, 0:4, :], r3(bank[2 * (t % 2)], 4), ACT.Copy).then_inc(s("h3t"), 1)
            e.wait_ge(s("top"), 1)
            e.activation(WT[:, 1, :], E1[:, :, :].rearrange("p a b -> p (a b)"), ACT.Exp).then_inc(s("e1"), 1)

            def split(gi, t0):
                for j in range(6):
                    m, q = divmod(j, 2)
                    if t0 is not None and q == 0:
                        e.wait_ge(s(("gate_pe", "up_pe", "y2_pe")[m]), t0 + (m == 2))
                    e.wait_ge(in_c[j], gi * 16 + 16)
                    e.activation(WH[m][:, q * RAW:q * RAW + RAW], RC[j][:, :], ACT.Copy).then_inc(s("m_hi"), 1)

            def rows_hi(t):
                for q in range(2):
                    e.wait_ge(s("et_pe"), t * 2 + q + 1)
                    e.activation(ETH[:, 4 * q:4 * q + 4, :], r3(bank[4 + q], 4), ACT.Copy).then_inc(s("et_hi"), 1)

            def result(t):
                waits(e, ("y2_pe", t + 1), ("y_st", t * 16 + 16))
                e.activation(YS[:, 0:512], bank[2], ACT.Copy).then_inc(s("ys_a"), 1)

            def tile(t):
                result(t)
                e.wait_ge(s("gate_pe"), t + 1)
                e.activation(SI[:, :], bank[0], ACT.Silu).then_inc(s("esilu"), 1)
                e.wait_ge(s("ht2_pe"), t + 1)
                e.activation(HTH[:, :, :], r3(bank[6], 4), ACT.Copy).then_inc(s("ht_hi"), 1)
                rows_hi(t + 1)
            e.wait_ge(s("cnt"), 1)
            e.wait_ge(s("scat"), 16 * 2 * NT)
            e.wait_ge(s("shared_st"), 16 * NT)
            rows_hi(0)
            split(0, None)
            with e.Fori(0, NE) as gi:
                n, t0 = group_of(e, gi)
                with e.Fori(0, n) as i:
                    tile(t0 + i)
                split(gi + 1, t0 + n)
            n, t0 = group_of(e, NE)
            with e.Fori(0, n) as i:
                tile(t0 + i)
            total = e.value_load(CNT[0:1, 31:32], min_val=NT + NE, max_val=MAXT)
            result(total)

        @blk.tensor
        def _(e):
            e.sem_inc(s("g_pe"), 1)
            e.wait_ge(s("const"), 14)
            for t in range(NT):
                e.wait_ge(s("xn"), t + 1)
                for q in range(2):
                    n = 2 * t + q
                    if n >= 4:
                        e.wait_ge(s("xt_lo"), n - 3)
                    for k in range(4):
                        m = e.transpose(bank[2 + n % 4][:, k * P:k * P + P],
                                        XN[t % 2][:, (4 * q + k) * P:(4 * q + k + 1) * P], IDF[:, :])
                    m.then_inc(s("xt_pe"), 1)
            e.wait_ge(s("ct_lo"), 1)
            e.wait_ge(free_a[0], 1)
            for n in range(2 * NT):
                t, q = divmod(n, 2)
                if n >= 4:
                    e.wait_ge(s(f"v_ev{n % 2}"), (n - 4) // 2 + 1)
                three(e, bank[VB[n % 4]], [(CTH[:, k, t * P:t * P + P], CTL[:, k, t * P:t * P + P],
                                            WVH[:, k, q * 512:q * 512 + 512], WVL[:, k, q * 512:q * 512 + 512])
                                           for k in range(KL)], True, True).then_inc(s("v_pe"), 1)
            e.wait_ge(s("v_ev0"), NT)
            e.wait_ge(s("v_ev1"), NT)
            e.wait_ge(s("xt_lo"), 2 * NT)

            def project(c, first):
                e.wait_ge(free_a[0], c + 2)
                if not first:
                    e.wait_ge(s("ot_lo"), 2 * c - 1)
                three(e, bank[6], [(WQH[:, k, :], WQL[:, k, :], XTH[:, k, :], XTL[:, k, :]) for k in range(KD)],
                      True, True).then_inc(s("q_pe"), 1)
                three(e, bank[7], [(WQH[:, KD + k, :], WQL[:, KD + k, :], CTH[:, k, :], CTL[:, k, :])
                                   for k in range(KL)], True, True).then_inc(s("k_pe"), 1)

            def scores(c):
                e.wait_ge(s("q_lo"), c + 1)
                e.wait_ge(s("k_lo"), c + 1)
                for h in range(2):
                    rows = slice(HD * h, HD * h + HD)
                    for i, off in HBLK:
                        w = P * (i + 1)
                        q = slice(i * P, i * P + P)
                        three(e, STR[h][:, off:off + w], [(QH[rows, q], QL[rows, q], KH[rows, 0:w], KLo[rows, 0:w])],
                              True, False)
                        m = e.matmul(STR[h][:, off + i * P:off + w], IDB[:, :], MASK[:, :], start=False, stop=True)
                    m.then_inc(s("s_pe"), 1)

            def attend(c, wait_banks):
                for h in range(2):
                    e.wait_ge(s("pn"), 2 * c - 1 + h)
                    for i, off in HBLK:
                        for j in range(i + 1):
                            at = TOFF[j] + (i - j) * P
                            m = e.transpose(STR[h][:, at:at + P], PR[h][:, off + j * P:off + j * P + P], IDF[:, :])
                    m.then_inc(s("t_pe"), 1)
                if wait_banks:
                    e.wait_ge(s("q_lo"), c + 1)
                    e.wait_ge(s("k_lo"), c + 1)
                e.wait_ge(s("vp_lo"), c)
                def part(h, V1, P1, first, last):
                    for j in range(NT):
                        off, w = TOFF[j], TOK - j * P
                        m = e.matmul(bank[6 + h][:, j * P:TOK], V1[:, j, :], P1[h][:, off:off + w],
                                     start=first and j == 0, stop=last and j == NT - 1)
                    return m
                for h in range(2):
                    e.wait_ge(s("pt_hi"), 2 * c - 1 + h)
                    part(h, VH, PTH, True, False)
                    part(h, VL, PTH, False, False)
                for h in range(2):
                    e.wait_ge(s("pt_lo"), 2 * c - 1 + h)
                    part(h, VH, PTL, False, True).then_inc(s("av_pe"), 1)
            project(0, True)
            scores(0)
            with e.Fori(1, NPAIR) as c:
                project(c, False)
                attend(c, True)
                scores(c)
            attend(NPAIR, False)
            e.wait_ge(s("ot_lo"), 2 * NPAIR + 1)
            for m in range(4):
                e.wait_ge(s("wo_lo"), m + 1)
                for kk in range(2):
                    k = 2 * m + kk
                    for t in range(NT):
                        for q in range(2):
                            cs = slice(q * 512, q * 512 + 512)
                            ins = three(e, bank[2 * t + q],
                                        [(OTH[:, k, t * P:t * P + P], OTL[:, k, t * P:t * P + P],
                                          WOH[m % 2][:, kk, cs], WOL[m % 2][:, kk, cs])], k == 0, k == KD - 1)
                ins.then_inc(s("y_pe"), 1)
            e.wait_ge(s("wsum"), 1)
            e.matmul(bank[0][:, 0:2], ONEF[:, :], WS[:, :], start=True, stop=True).then_inc(s("wsum_pe"), 1)

            for t in range(NT):
                e.wait_ge(s("zq"), t + 1)
                for k in range(KD):
                    m = e.transpose(bank[4 + t].bitcast(bf16)[:, k * P:k * P + P], ZQ[t % 2][:, k * P:k * P + P],
                                    IDB[:, :])
                m.then_inc(s("zt_pe"), 1)
            e.wait_ge(s("xq"), NT)
            e.wait_ge(s("z"), 1)

            def gate_group(c, p):
                e.wait_ge(s("tern"), c * 2 + 2)
                for t in range(NT):
                    e.wait_ge(s("h"), 4 * c + t + 1)
                    for k in range(KD):
                        m = e.matmul(bank[4 * p + t], XQ[:, k, t * P:t * P + P], TG[p][:, k, :],
                                     start=k == 0, stop=k == KD - 1)
                    m.then_inc(s("g_pe"), 1)
            with e.Fori(0, GC // 2) as it:
                gate_group(it * 2, 0)
                gate_group(it * 2 + 1, 1)
            gate_group(GC - 1, 0)
            e.wait_ge(s("h"), 8 + 4 * GC)

            def hidden_t(t):
                e.wait_ge(s("hq"), t + 1)
                for q, (k0, k1) in enumerate(HGRP):
                    if t:
                        e.wait_ge(s("hqt"), 3 * (t - 1) + q + 1)
                    for k in range(k0, k1):
                        m = e.transpose(bank[4 + q].bitcast(bf16)[:, (k - k0) * P:(k - k0 + 1) * P],
                                        HQ[:, k * P:k * P + P], IDB[:, :])
                    m.then_inc(s("ht_pe"), 1)

            hidden_t(0)
            for t in range(NT):
                e.wait_ge(s("hqt"), 3 * t + 3)
                if t >= 2:
                    e.wait_ge(s("x3"), t - 1)
                for q in range(2):
                    for k in range(KB):
                        if t == 0 and q == 0 and k % 2 == 0:
                            e.wait_ge(s("tern"), 2 * GC + k // 2 + 1)
                        m = e.matmul(bank[2 * (t % 2) + q], HQT[t % 2][:, k, :], TD[:, k, q * 512:q * 512 + 512],
                                     start=k == 0, stop=k == KB - 1)
                    m.then_inc(s("d_pe"), 1)
                    if q == 0 and t + 1 < NT:
                        hidden_t(t + 1)

            for t in range(NT):
                e.wait_ge(s("h3"), t + 1)
                if t >= 2:
                    e.wait_ge(s("h3t"), 2 * (t - 1))
                for q in range(2):
                    for k in range(4):
                        m = e.transpose(bank[2 * (t % 2) + q][:, k * P:k * P + P],
                                        H3[:, t, (4 * q + k) * P:(4 * q + k + 1) * P], IDF[:, :])
                    m.then_inc(s("h3t_pe"), 1)
                e.wait_ge(s("h3t"), 2 * t + 2)
                e.wait_ge(s("norm_in"), 64)
                for k in range(KD):
                    m = e.matmul(bank[4][:, 8 * t:8 * t + 8], H3T[:, k, :], WR[:, k, :],
                                 start=k == 0, stop=k == KD - 1)
                m.then_inc(s("lg_pe"), 1)
            e.wait_ge(s("slots_m"), 1)
            for t in range(NT):
                for u in range(t + 1):
                    e.matmul(bank[5][:, 8 * t:8 * t + 8], (TRI if u == t else ONEB)[:, :], MSB[:, u, :],
                             start=u == 0, stop=u == t)
            for t in range(NT):
                m = e.matmul(bank[5][:, 32:40], ONEB[:, :], MSB[:, t, :], start=t == 0, stop=t == NT - 1)
            m.then_inc(s("pos_pe"), 1)

            def rows_t(t, q):
                if q == 0:
                    e.wait_ge(s("e_in"), t * 16 + 16)
                for k in range(4):
                    m = e.transpose(bank[4 + q][:, k * P:k * P + P], XG[:, (4 * q + k) * P:(4 * q + k + 1) * P],
                                    IDF[:, :])
                m.then_inc(s("et_pe"), 1)

            def tile(t, gi):
                waits(e, ("et_hi", t * 2 + 2), (free_c[0], gi + 1), (free_c[1], gi + 1))
                for m in range(2):
                    if m:
                        waits(e, (free_c[2], gi + 1), (free_c[3], gi + 1))
                    highs(e, bank[m], [(ETH[:, k, :], WH[m][:, k * FE:k * FE + FE], WL[m][:, k * FE:k * FE + FE])
                                       for k in range(KD)])
                    e.wait_ge(s("et_lo"), t * 2 + 2)
                    lows(e, bank[m], [(ETL[:, k, :], WH[m][:, k * FE:k * FE + FE]) for k in range(KD)])\
                        .then_inc(s(("gate_pe", "up_pe")[m]), 1)
                rows_t(t + 1, 0)
                e.wait_ge(s("eh"), t + 1)
                for k in range(KE):
                    m = e.transpose(bank[6][:, k * P:k * P + P], HE[:, k * P:k * P + P], IDF[:, :])
                m.then_inc(s("ht2_pe"), 1)
                rows_t(t + 1, 1)
                waits(e, ("ht_hi", t + 1), ("ys_a", t + 1), ("ys_d", t + 1), (free_c[4], gi + 1), (free_c[5], gi + 1))

                def at(k, q):
                    return slice(k * DM + q * 512, k * DM + q * 512 + 512)
                for q in range(2):
                    highs(e, bank[2 + q], [(HTH[:, k, :], WH[2][:, at(k, q)], WL[2][:, at(k, q)])
                                           for k in range(KE)])
                e.wait_ge(s("ht_lo"), t + 1)
                for q in range(2):
                    m = lows(e, bank[2 + q], [(HTL[:, k, :], WH[2][:, at(k, q)]) for k in range(KE)])
                m.then_inc(s("y2_pe"), 1)
            e.wait_ge(s("cnt"), 1)
            for q in range(2):
                m = e.matmul(bank[2 + q][:, 0:512], IDF[:, :], XRES[:, 0, 0:512], start=True, stop=True)
            m.then_inc(s("y2_pe"), 1)
            rows_t(0, 0)
            rows_t(0, 1)
            with e.Fori(0, NE) as gi:
                n, t0 = group_of(e, gi)
                with e.Fori(0, n) as i:
                    tile(t0 + i, gi)
            n, t0 = group_of(e, NE)
            with e.Fori(0, n) as i:
                tile(t0 + i, NE)


def kernel(**inputs):
    import numpy as np
    import concourse.bacc as bacc
    from concourse.bass_utils import run_bass_kernel_spmd

    g = {k: np.asarray(v) for k, v in inputs.items()}

    def chunks(wt, n_out):
        k, o = wt.shape
        return wt.reshape(k // P, P, o // n_out, n_out).transpose(2, 1, 0, 3)

    def halves(a):
        n, p, w = a.shape
        return a.reshape(n, p, w // RAW, RAW).transpose(0, 2, 1, 3).reshape(-1, p, RAW)

    wkv = g["L0_xattn_Wkv_expand"]
    wq_c = chunks(g["L0_xattn_Wq"].T, P).reshape(NPAIR, P, KD * P)
    wk_c = chunks(wkv[:DM].T, P).reshape(NPAIR, P, KL * P)
    wg = g["L0_attn_w_gate"]
    gate_up = np.concatenate([wg[:FB].T.reshape(DM, GC, 1, GW), wg[FB:].T.reshape(DM, GC, 1, GW)], axis=2)
    gate_c = halves(chunks(gate_up.reshape(DM, 2 * FB), 2 * GW).reshape(GC, P, KD * 2 * GW))
    down_c = g["L0_attn_w_down"].T.reshape(GC, 2, P, DM).transpose(0, 2, 1, 3).reshape(GC, P, RAW)

    def expert(wgate, wup, wdown):
        def rows(a, k):
            return a.reshape(k, P, -1).transpose(1, 0, 2).reshape(1, P, 2 * RAW)
        return [halves(rows(wgate, KD)), halves(rows(wup, KD)), halves(rows(wdown, KE))]

    moe = expert(g["L0_ffn_sw_gate"], g["L0_ffn_sw_up"], g["L0_ffn_sw_down"])
    for k in range(NE):
        moe += expert(g["L0_ffn_w_gate"][k], g["L0_ffn_w_up"][k], g["L0_ffn_w_down"][k])
    arrays = {
        "x": g["x"][0],
        "ctxT": g["ctx_512"][0, :TOK].T.reshape(KL, P, TOK).transpose(1, 0, 2),
        "wv": wkv[DM:].T.reshape(KL, P, DM).transpose(1, 0, 2).reshape(P, RAW),
        "wqk": np.concatenate([wq_c, wk_c], axis=2),
        "wo": g["L0_xattn_Wout"].T.reshape(4, 2, P, DM).transpose(0, 2, 1, 3).reshape(4, P, RAW),
        "wbit": np.concatenate([gate_c, down_c], axis=0),
        "n_gate": g["L0_attn_norm_gate"], "n_down": g["L0_attn_norm_down"], "n_rms": g["L0_ffn_rms_weight"],
        "wrt": g["L0_ffn_router_w"].reshape(KD, P, NE).transpose(1, 0, 2),
        "wmoe": np.concatenate(moe, axis=0),
    }
    arrays = {k: np.ascontiguousarray(v) for k, v in arrays.items()}
    nc = bacc.Bacc("TRN2", target_bir_lowering=False, num_devices=1)
    args = [nc.dram_tensor(n, v.shape, mybir.dt.from_np(v.dtype), kind="ExternalInput").ap()
            for n, v in arrays.items()]
    out = nc.dram_tensor("out", (TOK, DM), f32, kind="ExternalOutput").ap()
    rows = nc.dram_tensor("rows", (DRAM_TILES * P, DM), f32, kind="Internal").ap()
    program(nc, *args, out, rows)
    r = run_bass_kernel_spmd(nc, [arrays], core_ids=[0])
    return r.results[0]["out"].reshape(1, TOK, DM)
```

```python
from contextlib import ExitStack

import concourse.bass as bass
from concourse import mybir

P = 128
TOK, DM, LAT = 512, 1024, 256
NT = TOK // P
KD = DM // P
KL = LAT // P
NH, HD = 16, 64
NPAIR = NH // 2
FB, KB = 2816, 22
GC, GW = 11, 256
NE, FE, KE = 8, 512, 4
NGRP = NE + 1
RAW = 2048
NABS = 2 * GC + GC
ABSP = 4
MAXT = NT + (2 * TOK // P + NE - 1)
XT_TILES = MAXT + 2
BLK0 = NT - 1
GATHER = (XT_TILES - BLK0) * P
DRAM_TILES = MAXT + NT + 2
HB3 = ((0, 1), (5, 6))
VB = (6, 7, 0, 1)
WO_SLOTS = (0, 2, 3, 4)
HGRP = ((0, 8), (8, 16), (16, 22))
MAGIC = 12582912.0
HBLK = [(3, 0), (2, 512), (0, 896), (1, 1024)]
SOFF = dict(HBLK)
TBLK = [(0, 0), (1, 512), (3, 896), (2, 1024)]
TOFF = dict(TBLK)
STRIP = 1280

f32, f32r, bf16 = mybir.dt.float32, mybir.dt.float32r, mybir.dt.bfloat16
i32, u32 = mybir.dt.int32, mybir.dt.uint32
ALU, ACT, AX = mybir.AluOpType, mybir.ActivationFunctionType, mybir.AxisListType


def program(nc, x, ctxT, wv, wqk, wo, wbit, n_gate, n_down, n_rms, wrt, wmoe, out, rows_dram):
    es = ExitStack()
    with es:
        sem_names = []

        def sem(name):
            sem_names.append(name)
            return es.enter_context(nc.semaphore(name))

        base = (nc.sbuf_base + 63) // 64 * 64

        class Region:
            def __init__(self, at):
                self.at = at

            def __call__(self, name, shape, dt):
                n = 2 if dt == bf16 else 4
                for s in shape[1:]:
                    n *= s
                t = nc.alloc_sbuf_tensor_at(name, shape, dt, offset=self.at)
                self.at += (n + 31) // 32 * 32
                assert self.at <= nc.sbuf_usable_end, (name, self.at)
                return t

        keep = Region(base)
        XRES = keep("XRES", [P, NT, DM], f32)
        IDF = keep("IDF", [P, P], f32)
        IDB = keep("IDB", [P, P], bf16)
        MASK = keep("MASK", [P, P], bf16)
        TRI = keep("TRI", [P, P], bf16)
        ONEB = keep("ONEB", [P, P], bf16)
        ONEF = keep("ONEF", [P, P], f32)
        CST = keep("CST", [P, 4], f32)
        BN = keep("BN", [P, NT, 2, 6], f32)
        MV = keep("MV", [P, NT, 2], f32)
        SM = keep("SM", [P, 128], f32)
        ACCW = keep("ACCW", [P, NABS], f32)
        IOTA8 = keep("IOTA8", [P, 8], f32)
        CNT = keep("CNT", [1, 32], i32)
        SLOT = keep("SLOT", [P, 2, NT], i32)
        RT = keep("RT", [P, 512], f32)
        M0B = keep("M0B", [P, 2, NT, 8], bf16)
        MSB = keep("MSB", [P, NT, 8], bf16)
        I8 = keep("I8", [P, NT, 8], u32)
        NM = RT[:, 0:8].rearrange("p (a b) -> p a b", a=2)
        RS = RT[:, 8:16].rearrange("p (a b) -> p a b", a=2)
        RSI = RT[:, 16:24].rearrange("p (a b) -> p a b", a=2)
        WS = RT[:, 24:26]
        MC = RT[:, 26:28]
        SW = RT[:, 28:30]
        E1 = RT[:, 32:36].rearrange("p (a b) -> p a b", b=1)
        WT = RT[:, 36:48].rearrange("p (a b) -> p a b", b=NT)
        LG = RT[:, 64:96].rearrange("p (a b) -> p a b", b=8)
        M8 = RT[:, 96:128].rearrange("p (a b) -> p a b", b=8)
        I8F = RT[:, 128:160].rearrange("p (a b) -> p a b", b=8)
        CTF = RT[:, 160:192]
        NEF = RT[:, 192:200]
        AT = RT[:, 200:232].rearrange("p (a b) -> p a b", b=8)
        SLM = RT[:, 232:296].rearrange("p (k t e) -> p k t e", k=2, t=NT)
        SLF = RT[:, 296:304]
        WR = keep("WR", [P, KD, 8], f32)
        start = keep.at

        a = Region(start)
        XTH = a("XTH", [P, KD, TOK], f32r)
        XTL = a("XTL", [P, KD, TOK], f32r)
        CTH = a("CTH", [P, KL, TOK], f32r)
        CTL = a("CTL", [P, KL, TOK], f32r)
        OTH = a("OTH", [P, KD, TOK], f32r)
        OTL = a("OTL", [P, KD, TOK], f32r)
        WQH = a("WQH", [P, KD + KL, P], f32r)
        WQL = a("WQL", [P, KD + KL, P], f32r)
        QH = a("QH", [P, TOK], f32r)
        QL = a("QL", [P, TOK], f32r)
        KH = a("KH", [P, TOK], f32r)
        KLo = a("KLo", [P, TOK], f32r)
        VH = a("VH", [P, NT, P], f32r)
        VL = a("VL", [P, NT, P], f32r)
        PTH = [a(f"PTH{h}", [P, STRIP], f32r) for h in range(2)]
        PTL = [a(f"PTL{h}", [P, STRIP], f32r) for h in range(2)]
        V = a("V", [P, NT, DM], f32)
        PR = [a(f"PR{h}", [P, STRIP], f32) for h in range(2)]
        RA = [a(f"RA{j}", [P, RAW], f32) for j in range(5)]
        CTX = nc.alloc_sbuf_tensor_at("CTX", [P, KL, TOK], f32, offset=V.manual_sbuf_range[0])
        WVH = nc.alloc_sbuf_tensor_at("WVH", [P, KL, DM], f32r, offset=OTH.manual_sbuf_range[0])
        WVL = nc.alloc_sbuf_tensor_at("WVL", [P, KL, DM], f32r, offset=OTL.manual_sbuf_range[0])
        XN = [nc.alloc_sbuf_tensor_at(f"XN{h}", [P, DM], f32, offset=PR[h].manual_sbuf_range[0]) for h in range(2)]
        w = Region(XTH.manual_sbuf_range[0])
        WOH = [w(f"WOH{s}", [P, 2, DM], f32r) for s in range(2)]
        WOL = [w(f"WOL{s}", [P, 2, DM], f32r) for s in range(2)]

        b = Region(start)
        XQ = b("XQ", [P, KD, TOK], bf16)
        TG = [b(f"TG{s}", [P, KD, 2 * GW], bf16) for s in range(2)]
        TD = b("TD", [P, KB, DM], bf16)
        HQ = b("HQ", [P, FB], bf16)
        HQT = [b(f"HQT{s}", [P, KB, P], bf16) for s in range(2)]
        HB = b("HB", [P, NT, FB], f32)
        SG = b("SG", [P, NT, GW], f32)
        NG = b("NG", [P, DM], f32)
        ND = b("ND", [P, FB], f32)
        c = Region(start)
        WH = [c(f"WH{m}", [P, RAW * 2], f32r) for m in range(3)]
        WL = [None] + [c(f"WL{m}", [P, RAW * 2], f32r) for m in (1, 2)]
        ETH = c("ETH", [P, KD, P], f32r)
        ETL = c("ETL", [P, KD, P], f32r)
        WL[0] = c("WL0", [P, RAW * 2], f32r)
        HTH = c("HTH", [P, KE, P], f32r)
        HTL = c("HTL", [P, KE, P], f32r)
        SI = c("SI", [P, FE], f32)
        HE = c("HE", [P, FE], f32)
        XG = c("XG", [P, DM], f32)
        YS = c("YS", [P, DM], f32)
        RC = [c(f"RC{j}", [P, RAW], f32) for j in (4, 5)]
        H3 = c("H3", [P, NT, DM], f32)
        b.at = max(b.at, c.at)
        RB = [b(f"RB{j}", [P, RAW], f32) for j in range(4)]
        RC = [nc.alloc_sbuf_tensor_at(f"RC{j}", [P, RAW], f32, offset=RB[j].manual_sbuf_range[0])
              for j in range(4)] + RC
        ZERO = nc.alloc_sbuf_tensor_at("ZERO", [P, DM], f32, offset=SG.manual_sbuf_range[0])
        JB = nc.alloc_sbuf_tensor_at("JB", [P, FB], bf16, offset=TG[0].manual_sbuf_range[0])
        JB0 = nc.alloc_sbuf_tensor_at("JB0", [P, FB - GW], bf16, offset=HQ.manual_sbuf_range[0])
        z = Region(HB.manual_sbuf_range[0])
        Z = z("Z", [P, NT, DM], f32)
        ZQ = [z(f"ZQ{s}", [P, DM], bf16) for s in range(2)]
        ZJ = z("ZJ", [P, DM], f32)

        r = Region(TG[1].manual_sbuf_range[0])
        NR = r("NR", [P, DM], f32)
        H3T = r("H3T", [P, KD, P], f32)
        g = Region(WH[0].manual_sbuf_range[0])
        GA = g("GA", [P, NT, DM], f32)
        GB = g("GB", [P, NT, DM], f32)

        BK = [es.enter_context(nc.psum_tensor(f"BK{i}", [P, 1536 if i in (0, 3) else 512], f32))
              for i in (0, 3, 6, 7)]
        STR = BK[0:2]
        bank = [BK[i // 3][:, i % 3 * 512:i % 3 * 512 + 512] if i < 6 else BK[i - 4][:, :] for i in range(8)]

        S = {}

        def s(name):
            if name not in S:
                S[name] = sem(name)
            return S[name]

        for n in ("const", "v_eps", "sqrt", "ln",
                  "x_in0", "x_in1", "x_in2", "x_in3", "ctx_in", "norm_in",
                  "xn", "xt_pe", "xt_hi", "xt_lo", "ct_hi", "ct_lo", "wv_hi", "v_pe", "v_ev0", "v_ev1",
                  "wq_hi", "q_pe", "k_pe", "q_hi", "q_lo", "k_hi", "k_lo", "vp_hi", "vp_lo", "s_pe",
                  "nmax", "exp", "rsum", "pn", "t_pe", "pt_hi", "pt_lo", "av_pe", "ot_hi", "ot_lo", 
                  "wo_hi", "wo_lo", "y_pe", "x2",
                  "y_tile", "hnd", "hrnd", "zrnd", "wsum", "wsum_pe", "wscale", "z", "zq", "zt_pe", "xq",
                  "rnd", "tern", "g_pe", "silu", "h", "h_sq0", "h_sq", "hz", "hq", "ht_pe", "hqt", "d_pe", "x3",
                  "h3", "h3t_pe", "h3t", "lg_pe", "top", "e1", "pos_pe", "cnt", "slots", "scat", "zero_in", "zero",
                  "dself",
                  "slots_m", "rows", "y_all", "m_hi", "e_in", "et_pe", "et_hi", "et_lo", "gate_pe", "up_pe", "esilu", "eh", "ht2_pe",
                  "ht_hi", "ht_lo", "y2_pe", "ys_a", "ys_d", "y_st", "fin_in0", "fin_in1", "fin_in2", "fin_in3", "fin", "out"):
            s(n)
        in_a = [sem(f"raw_a{j}") for j in range(5)]
        free_a = [sem(f"free_a{j}") for j in range(5)]
        in_b = [sem(f"raw_b{j}") for j in range(4)]
        free_b = [sem(f"free_b{j}") for j in range(4)]
        in_c = [sem(f"raw_c{j}") for j in range(6)]
        free_c = [sem(f"free_c{j}") for j in range(6)]

        blk = es.enter_context(nc.Block())

        def r3(ap, n):
            return ap.rearrange("p (a b) -> p a b", a=n)

        def three(e, dst, pairs, first, last):
            m, n = None, len(pairs)
            for i, (sh, sl, mh, ml) in enumerate(pairs):
                for j, (st, mv) in enumerate(((sh, mh), (sh, ml), (sl, mh))):
                    m = e.matmul(dst, st, mv, start=first and i == 0 and j == 0, stop=last and i == n - 1 and j == 2)
            return m

        def highs(e, dst, pairs, first=True):
            for i, (sh, mh, ml) in enumerate(pairs):
                e.matmul(dst, sh, mh, start=first and i == 0, stop=False)
                e.matmul(dst, sh, ml, start=False, stop=False)

        def lows(e, dst, pairs):
            for i, (sl, mh) in enumerate(pairs):
                m = e.matmul(dst, sl, mh, start=False, stop=i == len(pairs) - 1)
            return m

        class Own:
            def __init__(self, e, name):
                self.e, self.sem, self.n = e, s(name), 0

            def __call__(self, ins):
                ins.then_inc(self.sem, 1)
                self.n += 1
                self.e.wait_ge(self.sem, self.n)

        own = {}

        def col(k):
            return SM[:, 4 * k:4 * k + 4]

        def inv_sqrt(e, v, q, dst, sync_value):
            o = own["dve"]
            e.wait_ge(s("sqrt"), sync_value)
            t = col(14)[:, 0:v.shape[1]]
            o(e.reciprocal(dst, q))
            o(e.tensor_tensor(t, dst, dst, ALU.mult))
            o(e.tensor_tensor(t, t, v, ALU.mult))
            o(e.tensor_scalar(t, t, -0.5, 1.5, ALU.mult, ALU.add))
            o(e.tensor_tensor(dst, dst, t, ALU.mult))

        def group_of(e, gi):
            e_n = CNT[0:1, bass.ds(gi, 1)] if not isinstance(gi, int) else CNT[0:1, gi:gi + 1]
            e_t = CNT[0:1, bass.ds(gi + 10, 1)] if not isinstance(gi, int) else CNT[0:1, gi + 10:gi + 11]
            return e.value_load(e_n, min_val=1, max_val=NT), e.value_load(e_t, min_val=NT, max_val=MAXT - 1)

        def waits(e, *pairs):
            at = [(s(n) if isinstance(n, str) else n, v if isinstance(v, int) else e.snap(v)) for n, v in pairs]
            for sm, v in at:
                e.wait_ge(sm, v)

        roots = [0]

        def root(e, v, q):
            roots[0] += 1
            e.wait_ge(s("v_eps"), roots[0])
            e.activation(q, v, ACT.Sqrt).then_inc(s("sqrt"), 1)

        veps = [0]

        def layer_norm_stats(e):
            o = own["dve"]
            for t in range(NT):
                if veps[0] == 0:
                    e.wait_ge(s(f"x_in{t}"), 16)
                for h in range(2):
                    ins = e.bn_stats(BN[:, t, h, :], XRES[:, t, h * 512:h * 512 + 512])
                o(ins)
                o(e.bn_aggr(MV[:, t, :], BN[:, t, :, :].rearrange("p a b -> p (a b)")))
            e.tensor_scalar(col(2), MV[:, :, 1:2].rearrange("p a b -> p (a b)"), 1e-5, None, ALU.add)\
                .then_inc(s("v_eps"), 1)
            veps[0] += 1
            e.wait_ge(s("v_eps"), veps[0])
            inv_sqrt(e, col(2), col(3), col(0), veps[0])
            e.scalar_tensor_tensor(out=col(1), in0=MV[:, :, 0:1].rearrange("p a b -> p (a b)"), scalar=-1.0,
                                   in1=col(0), op0=ALU.mult, op1=ALU.mult).then_inc(s("ln"), 1)

        def tile_stats(e, t, eps):
            o = own["dve"]
            for h in range(2):
                ins = e.bn_stats(BN[:, t, h, :], XRES[:, t, h * 512:h * 512 + 512])
            o(ins)
            o(e.bn_aggr(MV[:, t, :], BN[:, t, :, :].rearrange("p a b -> p (a b)")))
            one = slice(t, t + 1)
            e.tensor_scalar(col(1)[:, one], MV[:, t, 0:1], -1.0, None, ALU.mult)
            o(e.tensor_scalar(col(2)[:, one], MV[:, t, 1:2], 1e-5, eps, ALU.add, ALU.mult))
            o(e.tensor_tensor(col(2)[:, one], col(2)[:, one], MV[:, t, 1:2], ALU.add))

        @blk.sync
        def _(e):
            e.dma_start(CTX[:, :, :], ctxT).then_inc(s("ctx_in"), 16)
            e.dma_start(RA[0][:, :], wv).then_inc(in_a[0], 16)
            for t in range(NT):
                e.dma_start(XRES[:, t, :], x[t * P:t * P + P, :]).then_inc(s(f"x_in{t}"), 16)

            def qk_load(c):
                e.wait_ge(free_a[0], c + 1)
                src = wqk[c] if isinstance(c, int) else wqk[bass.ds(c, 1), :, :].rearrange("a p n -> p (a n)")
                e.dma_start(RA[0][:, 0:STRIP], src).then_inc(in_a[0], 16)

            def sum_loads(c, first):
                for j in range(1, 5):
                    if not first:
                        e.wait_ge(free_a[j], c)
                    e.dma_start(RA[j][:, :], wbit[bass.ds(c * ABSP + j - 1, 1), :, :]
                                .rearrange("a p n -> p (a n)")).then_inc(in_a[j], 16)
            qk_load(0)
            sum_loads(0, True)
            qk_load(1)
            with e.Fori(1, NPAIR - 1) as c:
                qk_load(c + 1)
                sum_loads(c, False)
            sum_loads(NPAIR - 1, False)
            for m, j in enumerate(WO_SLOTS):
                e.wait_ge(free_a[j], NPAIR + 1 if j == 0 else NPAIR)
                e.dma_start(RA[j][:, :], wo[m]).then_inc(in_a[j], 16)
            e.wait_ge(free_a[1], NPAIR)
            e.dma_start(RA[1][:, :], wbit[NABS - 1]).then_inc(in_a[1], 16)

            e.wait_ge(s("ot_lo"), 2 * NPAIR + 1)
            e.wait_ge(s("wo_lo"), 1)
            e.dma_start(NG[:, :], n_gate.partition_broadcast(P)).then_inc(s("norm_in"), 16)
            e.dma_start(ND[:, :], n_down.partition_broadcast(P)).then_inc(s("norm_in"), 16)
            e.dma_start(WR[:, :, :], wrt).then_inc(s("norm_in"), 16)

            def bit_load(j, chunk, waits):
                if waits is not None:
                    e.wait_ge(free_b[j], waits)
                src = wbit[chunk] if isinstance(chunk, int) else \
                    wbit[bass.ds(chunk, 1), :, :].rearrange("a p n -> p (a n)")
                e.dma_start(RB[j][:, :], src).then_inc(in_b[j], 16)
            e.wait_ge(free_a[1], NPAIR + 1)
            for j in range(4):
                e.wait_ge(s("wo_lo"), min(j + 2, 4))
                bit_load(j, j, None)
            with e.Fori(1, 8) as k:
                for j in range(4):
                    bit_load(j, k * 4 + j, k)
            bit_load(0, NABS - 1, 8)

            e.wait_ge(s("h"), 8 + 4 * GC)
            e.dma_start(NR[:, :], n_rms.partition_broadcast(P)).then_inc(s("norm_in"), 16)

            def group_loads(gi, first):
                for j in range(6):
                    if first and j < 4:
                        e.wait_ge(free_b[j], 9 if j == 0 else 8)
                    elif first:
                        e.wait_ge(s("hq"), NT)
                    else:
                        e.wait_ge(free_c[j], gi)
                    e.dma_start(RC[j][:, :], wmoe[bass.ds(gi * 6 + j, 1), :, :].rearrange("a p n -> p (a n)"))\
                        .then_inc(in_c[j], 16)
            group_loads(0, True)
            group_loads(1, False)
            e.sem_inc(s("e_in"), 16 * NT)
            e.wait_ge(s("rows"), 1)
            e.dma_start(XG[:, :], rows_dram[P:2 * P, :]).then_inc(s("e_in"), 16)
            e.wait_ge(s("et_pe"), 2 * NT + 2)
            e.dma_start(XG[:, :], rows_dram[2 * P:3 * P, :]).then_inc(s("e_in"), 16)
            e.sem_inc(s("y_st"), 16 * (NT + 1))

            def tile(t):
                row, row2 = e.snap((t - NT) * P), e.snap((t - NT + 3) * P)
                waits(e, ("ys_a", t + 1), ("ys_d", t + 1), ("y_st", t * 16 + 16))
                e.dma_start(rows_dram[bass.ds(row, P), :], YS[:, :]).then_inc(s("y_st"), 16)
                e.wait_ge(s("et_pe"), t * 2 + 4)
                e.dma_start(XG[:, :], rows_dram[bass.ds(row2, P), :]).then_inc(s("e_in"), 16)
            e.wait_ge(s("cnt"), 1)
            with e.Fori(1, NE) as gi:
                group_loads(gi + 1, False)
                n, t0 = group_of(e, gi)
                with e.Fori(0, n) as i:
                    tile(t0 + i)
            n, t0 = group_of(e, NE)
            with e.Fori(0, n) as i:
                tile(t0 + i)
            total = e.value_load(CNT[0:1, 31:32], min_val=NT + NE, max_val=MAXT)
            row = e.snap((total - NT) * P)
            waits(e, ("ys_a", total + 1), ("ys_d", total + 1), ("y_st", total * 16 + 16))
            e.dma_start(rows_dram[bass.ds(row, P), :], YS[:, :]).then_inc(s("y_st"), 16)
            waits(e, ("y_st", total * 16 + 32), ("e_in", total * 16 + 32))
            e.sem_inc(s("y_all"), 1)

            for t in range(NT):
                e.wait_ge(s("fin"), t + 1)
                e.dma_start(out[t * P:t * P + P, :], XRES[:, t, :]).then_inc(s("out"), 16)
            e.wait_ge(s("out"), 16 * NT)

        @blk.gpsimd
        def _(e):
            for ins in (e.memset(IDF[:, :], 0.0), e.memset(IDB[:, :], 0.0), e.memset(MASK[:, :], 0.0),
                        e.memset(TRI[:, :], 1.0), e.memset(ONEB[:, :], 1.0), e.memset(ONEF[:, :], 1.0),
                        e.memset(CST[:, :], MAGIC),
                        e.iota(I8[:, 0, :], pattern=[[1, 8]], base=0, channel_multiplier=0)):
                ins.then_inc(s("const"), 1)
            e.wait_ge(s("const"), 8)
            for m in (IDF, IDB):
                e.affine_select(out=m[:, :], in_=m[:, :], compare_op=ALU.not_equal, fill=1.0, base=0,
                                pattern=[[-1, P]], channel_multiplier=1).then_inc(s("const"), 1)
            e.affine_select(out=MASK[:, :], in_=MASK[:, :], compare_op=ALU.is_ge, fill=-1e30, base=0,
                            pattern=[[-1, P]], channel_multiplier=1).then_inc(s("const"), 1)
            e.affine_select(out=TRI[:, :], in_=TRI[:, :], compare_op=ALU.is_gt, fill=0.0, base=0,
                            pattern=[[1, P]], channel_multiplier=-1).then_inc(s("const"), 1)
            e.tensor_copy(IOTA8[:, :], I8[:, 0, :]).then_inc(s("const"), 1)
            def w_lo(c):
                e.wait_ge(s("wq_hi"), c + 1)
                e.tensor_tensor(WQL[:, :, :].rearrange("p a b -> p (a b)"), RA[0][:, 0:STRIP],
                                WQH[:, :, :].rearrange("p a b -> p (a b)").bitcast(f32), ALU.subtract)\
                    .then_inc(free_a[0], 1)

            def v_lo(c):
                e.wait_ge(s("vp_hi"), c + 1)
                e.tensor_tensor(VL[:, :, :], V[:, :, bass.ds(c * P, P)], VH[:, :, :].bitcast(f32), ALU.subtract)\
                    .then_inc(s("vp_lo"), 1)
            w_lo(0)
            with e.Fori(1, NPAIR) as c:
                w_lo(c)
                v_lo(c - 1)
            v_lo(NPAIR - 1)
            e.wait_ge(s("ot_lo"), 2 * NPAIR + 1)
            e.memset(ZERO[:, :], 0.0).then_inc(s("zero_in"), 1)
            e.wait_ge(s("zero_in"), 1)
            for k in range(NT, XT_TILES):
                e.dma_start(rows_dram[(k - BLK0) * P:(k - BLK0 + 1) * P, :], ZERO[:, :]).then_inc(s("zero"), 16)
            for t in range(1, NT):
                e.wait_ge(s("h_sq"), t + 1)
                e.tensor_tensor(HB[:, t, :], HB[:, t, :], ND[:, :], ALU.mult).then_inc(s("hnd"), 1)

            e.wait_ge(s("slots"), 1)
            e.wait_ge(s("h3"), NT)
            e.wait_ge(s("zero"), 16 * (XT_TILES - NT))
            for k in range(2):
                for t in range(NT):
                    e.indirect_dma_start(rows_dram[0:GATHER, :], bass.IndirectOffsetOnAxis(ap=SLOT[:, k, t:t + 1], axis=0),
                                         H3[:, t, :], None).then_inc(s("scat"), 16)
            e.wait_ge(s("scat"), 16 * 2 * NT)
            e.sem_inc(s("rows"), 1)
            e.wait_ge(s("y_all"), 1)
            for t in range(NT):
                for k, dst in enumerate((GA, GB)):
                    e.indirect_dma_start(dst[:, t, :], None, rows_dram[0:GATHER, :],
                                         bass.IndirectOffsetOnAxis(ap=SLOT[:, k, t:t + 1], axis=0))\
                        .then_inc(s(f"fin_in{t}"), 16)

        @blk.vector
        def _(e):
            own["dve"] = o = Own(e, "dself")
            e.sem_inc(s("ot_lo"), 1)
            e.sem_inc(s("h"), 8)
            e.wait_ge(s("ct_hi"), 1)
            e.tensor_tensor(CTL[:, :, :], CTX[:, :, :], CTH[:, :, :].bitcast(f32), ALU.subtract)\
                .then_inc(s("ct_lo"), 1)
            e.wait_ge(s("wv_hi"), 1)
            e.tensor_tensor(WVL[:, :, :], r3(RA[0][:, :], 2), WVH[:, :, :].bitcast(f32), ALU.subtract)\
                .then_inc(free_a[0], 1)
            layer_norm_stats(e)
            for t in range(NT):
                e.wait_ge(s("v_pe"), 2 * t + 2)
                e.tensor_copy(V[:, t, 512:1024], bank[VB[(2 * t + 1) % 4]]).then_inc(s("v_ev1"), 1)
            for n in range(2 * NT):
                t, q = divmod(n, 2)
                e.wait_ge(s("xt_hi"), n + 1)
                e.tensor_tensor(XTL[:, 4 * q:4 * q + 4, t * P:t * P + P], r3(bank[2 + n % 4], 4),
                                XTH[:, 4 * q:4 * q + 4, t * P:t * P + P].bitcast(f32), ALU.subtract)\
                    .then_inc(s("xt_lo"), 1)

            def absum(j, column, n):
                e.wait_ge(in_a[j], n)
                e.tensor_reduce(ACCW[:, column], RA[j][:, :], AX.X, ALU.add, apply_absolute_value=True)\
                    .then_inc(free_a[j], 1)

            def close_pair(c):
                for h in range(2):
                    e.wait_ge(s("pt_hi"), 2 * c - 1 + h)
                    e.tensor_tensor(PTL[h][:, :], STR[h][:, 0:STRIP], PTH[h][:, :].bitcast(f32), ALU.subtract)\
                        .then_inc(s("pt_lo"), 1)
                for h in range(2):
                    rows = slice(HD * h, HD * h + HD)
                    e.wait_ge(s("ot_hi"), 2 * c - 1 + h)
                    e.tensor_tensor(OTL[rows, bass.ds(c - 1, 1), :].rearrange("p a n -> p (a n)"),
                                    bank[6 + h][rows, :],
                                    OTH[rows, bass.ds(c - 1, 1), :].rearrange("p a n -> p (a n)").bitcast(f32),
                                    ALU.subtract).then_inc(s("ot_lo"), 1)

            def pair(c, first):
                e.wait_ge(s("q_hi"), c + 1)
                e.scalar_tensor_tensor(out=QL[:, :], in0=bank[6], scalar=HD ** -0.5, in1=QH[:, :].bitcast(f32),
                                       op0=ALU.mult, op1=ALU.subtract).then_inc(s("q_lo"), 1)
                e.wait_ge(s("k_hi"), c + 1)
                e.tensor_tensor(KLo[:, :], bank[7], KH[:, :].bitcast(f32), ALU.subtract).then_inc(s("k_lo"), 1)
                if not first:
                    close_pair(c)
                for h in range(2):
                    e.wait_ge(s("s_pe"), 2 * c + h + 1)
                    for i, off in HBLK:
                        ins = e.tensor_reduce(NM[:, h, i:i + 1], STR[h][:, off:off + P * (i + 1)], AX.X, ALU.max,
                                              negate=True)
                    ins.then_inc(s("nmax"), 1)
                absum(2, bass.ds(c * ABSP + 1, 1), c * 16 + 16)
                for h in range(2):
                    e.wait_ge(s("exp"), 2 * c + h + 1)
                    e.reciprocal(RSI[:, h, :], RS[:, h, :]).then_inc(s("rsum"), 1)
                    e.wait_ge(s("rsum"), 2 * c + h + 1)
                    for i, off in HBLK:
                        v = PR[h][:, off:off + P * (i + 1)]
                        ins = e.tensor_scalar(v, v, RSI[:, h, i:i + 1], None, ALU.mult)
                    ins.then_inc(s("pn"), 1)
                absum(4, bass.ds(c * ABSP + 3, 1), c * 16 + 16)
            pair(0, True)
            with e.Fori(1, NPAIR) as c:
                pair(c, False)

            def wo_lo(m):
                j = WO_SLOTS[m]
                e.wait_ge(s("wo_hi"), m + 1)
                e.tensor_tensor(WOL[m % 2][:, :, :], r3(RA[j][:, :], 2), WOH[m % 2][:, :, :].bitcast(f32),
                                ALU.subtract).then_inc(s("wo_lo"), 1)
            wo_lo(0)
            close_pair(NPAIR)
            for m in range(1, 4):
                wo_lo(m)
            for j in (2, 4):
                e.wait_ge(free_a[j], NPAIR)
            e.wait_ge(free_a[1], NPAIR + 1)
            e.wait_ge(free_a[3], NPAIR)
            e.tensor_reduce(WS[:, 0:1], ACCW[:, 0:2 * GC], AX.X, ALU.add)
            e.tensor_reduce(WS[:, 1:2], ACCW[:, 2 * GC:NABS], AX.X, ALU.add).then_inc(s("wsum"), 1)
            e.wait_ge(s("norm_in"), 48)
            for t in range(NT):
                e.wait_ge(s("y_tile"), t + 1)
                for q in range(2):
                    v = XRES[:, t, q * 512:q * 512 + 512]
                    ins = e.tensor_tensor(v, bank[2 * t + q], v, ALU.add)
                ins.then_inc(s("x2"), 1)
                e.wait_ge(s("x2"), t + 1)
                tile_stats(e, t, 1e-8)
                o(e.scalar_tensor_tensor(out=Z[:, t, :], in0=XRES[:, t, :], scalar=col(1)[:, t:t + 1], in1=NG[:, :],
                                         op0=ALU.add, op1=ALU.mult))
                if t == NT - 1:
                    e.sem_inc(s("v_eps"), 1)
                    veps[0] += 1
                o(e.tensor_reduce(col(6)[:, t:t + 1], Z[:, t, :], AX.X, ALU.max, apply_absolute_value=True))
            e.wait_ge(s("wsum_pe"), 1)
            o(e.tensor_scalar(MC[:, 0:1], bank[0][:, 0:1], 1.0 / (2 * FB * DM), 1e-5, ALU.mult, ALU.max))
            o(e.tensor_scalar(MC[:, 1:2], bank[0][:, 1:2], 1.0 / (FB * DM), 1e-5, ALU.mult, ALU.max))
            e.reciprocal(SW[:, :], MC[:, :]).then_inc(s("wscale"), 1)
            inv_sqrt(e, col(2), col(3), col(5), veps[0])
            o(e.tensor_tensor(col(7), col(6), col(5), ALU.mult))
            o(e.tensor_scalar(col(7), col(7), 1e-5, None, ALU.max))
            o(e.reciprocal(col(8), col(7)))
            o(e.tensor_tensor(col(8), col(8), col(5), ALU.mult))
            o(e.tensor_scalar(col(8), col(8), 127.0, None, ALU.mult))
            e.tensor_scalar(col(9), col(7), MC[:, 0:1], 1.0 / 127.0, ALU.mult, ALU.mult).then_inc(s("z"), 1)
            for t in range(NT):
                if t < 2:
                    e.wait_ge(s("zrnd"), t + 1)
                else:
                    o(e.tensor_scalar(Z[:, t, :], Z[:, t, :], col(8)[:, t:t + 1], MAGIC, ALU.mult, ALU.add))
                    e.wait_ge(s("zt_pe"), t - 1)
                e.tensor_scalar(ZQ[t % 2][:, :], Z[:, t, :], -MAGIC, None, ALU.add).then_inc(s("zq"), 1)

            def ternary(dst, j, n, use):
                e.wait_ge(s("rnd"), n + 1)
                e.tensor_scalar(dst, RB[j][:, :], -MAGIC, 1.0, ALU.add, ALU.min).then_inc(free_b[j], 1)
                e.wait_ge(free_b[j], use)
                e.tensor_scalar(dst, dst, -1.0, None, ALU.max).then_inc(s("tern"), 1)

            def gate_weights(p, j0, n, use):
                for q in range(2):
                    ternary(TG[p][:, 4 * q:4 * q + 4, :].rearrange("p a b -> p (a b)"), j0 + q, n + q, use)

            def gate_group(c, p):
                for t in range(NT):
                    e.wait_ge(s("silu"), 4 * c + t + 1)
                    e.scalar_tensor_tensor(out=HB[:, t, bass.ds(c * GW, GW)], in0=bank[4 * p + t][:, GW:2 * GW],
                                           scalar=col(9)[:, t:t + 1], in1=SG[:, t, :],
                                           op0=ALU.mult, op1=ALU.mult).then_inc(s("h"), 1)
            gate_weights(0, 0, 0, 1)
            with e.Fori(0, GC // 2) as it:
                waits(e, ("g_pe", it * 8 + 1), ("rnd", it * 4 + 3))
                gate_weights(1, 2, it * 4 + 2, it + 1)
                gate_group(it * 2, 0)
                waits(e, ("g_pe", it * 8 + 5), ("rnd", it * 4 + 5))
                gate_weights(0, 0, it * 4 + 4, it + 2)
                gate_group(it * 2 + 1, 1)
            e.wait_ge(s("h_sq0"), 1)
            o(e.tensor_tensor(HB[:, 0, 0:FB - GW], HB[:, 0, 0:FB - GW], ND[:, 0:FB - GW], ALU.mult))
            o(e.tensor_reduce(col(16)[:, 0:1], HB[:, 0, 0:FB - GW], AX.X, ALU.max, apply_absolute_value=True))
            gate_group(GC - 1, 0)

            def hidden_quant(t):
                one = slice(t, t + 1)
                e.wait_ge(s("h_sq"), t + 1)
                if t == 0:
                    o(e.tensor_tensor(col(10)[:, 0:1], col(10)[:, 0:1], col(17)[:, 0:1], ALU.add))
                e.tensor_scalar(col(4)[:, one], col(10)[:, one], 1.0 / FB, 1e-8, ALU.mult, ALU.add)\
                    .then_inc(s("v_eps"), 1)
                veps[0] += 1
                if t:
                    e.wait_ge(s("hnd"), t)
                else:
                    o(e.tensor_tensor(HB[:, 0, FB - GW:FB], HB[:, 0, FB - GW:FB], ND[:, FB - GW:FB], ALU.mult))
                at = slice(0, FB) if t else slice(FB - GW, FB)
                o(e.tensor_reduce(col(11)[:, one], HB[:, t, at], AX.X, ALU.max, apply_absolute_value=True))
                if t == 0:
                    o(e.tensor_tensor(col(11)[:, one], col(11)[:, one], col(16)[:, one], ALU.max))
                e.wait_ge(s("v_eps"), veps[0])
                inv_sqrt(e, col(4)[:, one], col(3)[:, one], col(12)[:, one], veps[0])
                o(e.tensor_scalar(col(13)[:, one], col(11)[:, one], col(12)[:, one], 1e-5, ALU.mult, ALU.max))
                o(e.reciprocal(col(6)[:, one], col(13)[:, one]))
                o(e.tensor_scalar(col(6)[:, one], col(6)[:, one], col(12)[:, one], 127.0, ALU.mult, ALU.mult))
                e.tensor_scalar(col(8)[:, one], col(13)[:, one], MC[:, 1:2], 1.0 / 127.0, ALU.mult, ALU.mult)
                e.wait_ge(s("dself"), o.n)
                e.sem_inc(s("hz"), 1)

            def hidden_integers(t):
                e.wait_ge(s("hrnd"), t + 1)
                if t:
                    e.wait_ge(s("ht_pe"), 3 * t)
                e.tensor_scalar(HQ[:, :], HB[:, t, :], -MAGIC, None, ALU.add).then_inc(s("hq"), 1)

            def down_weights(i0, i1):
                for i in range(i0, i1):
                    n = 2 * GC + i
                    ternary(TD[:, 2 * i:2 * i + 2, :].rearrange("p a b -> p (a b)"), n % 4, n, n // 4 + 1)

            def second_residual(t):
                for q in range(2):
                    v = XRES[:, t, q * 512:q * 512 + 512]
                    e.wait_ge(s("d_pe"), 2 * t + q + 1)
                    ins = e.scalar_tensor_tensor(out=v, in0=bank[2 * (t % 2) + q], scalar=col(8)[:, t:t + 1], in1=v,
                                                 op0=ALU.mult, op1=ALU.add)
                ins.then_inc(s("x3"), 1)
            def split(gi, m):
                for q in range(2):
                    j = 2 * m + q
                    e.wait_ge(s("m_hi"), gi * 6 + j + 1)
                    e.tensor_tensor(WL[m][:, q * RAW:q * RAW + RAW], RC[j][:, :],
                                    WH[m][:, q * RAW:q * RAW + RAW].bitcast(f32), ALU.subtract)\
                        .then_inc(free_c[j], 1)

            def rows_lo(t):
                for q in range(2):
                    e.wait_ge(s("et_hi"), t * 2 + q + 1)
                    e.tensor_tensor(ETL[:, 4 * q:4 * q + 4, :], r3(bank[4 + q], 4),
                                    ETH[:, 4 * q:4 * q + 4, :].bitcast(f32), ALU.subtract).then_inc(s("et_lo"), 1)

            def hidden(t):
                waits(e, ("esilu", t + 1), ("up_pe", t + 1))
                e.tensor_tensor(HE[:, :], bank[1], SI[:, :], ALU.mult).then_inc(s("eh"), 1)
                e.wait_ge(s("ht_hi"), t + 1)
                e.tensor_tensor(HTL[:, :, :], r3(bank[6], 4), HTH[:, :, :].bitcast(f32), ALU.subtract)\
                    .then_inc(s("ht_lo"), 1)

            def shared_tile(t):
                hidden(t)
                rows_lo(t + 1)

            def shared_result(t):
                e.wait_ge(s("y2_pe"), t + 2)
                for q in range(2):
                    v = XRES[:, t, q * 512:q * 512 + 512]
                    ins = e.tensor_tensor(v, bank[2 + q], v, ALU.add)
                ins.then_inc(s("ys_d"), 1)

            def result(t):
                waits(e, ("y2_pe", t + 1), ("y_st", t * 16 + 16))
                e.tensor_copy(YS[:, 512:1024], bank[3]).then_inc(s("ys_d"), 1)

            def router_evac(t):
                e.wait_ge(s("h3t_pe"), 2 * t + 2)
                if t:
                    e.wait_ge(s("lg_pe"), t)
                e.tensor_copy(H3T[:, 4:8, :], r3(bank[HB3[t % 2][1]], 4)).then_inc(s("h3t"), 1)

            def router_rows(t):
                one = slice(t, t + 1)
                tile_stats(e, t, 1e-6)
                e.sem_inc(s("v_eps"), 1)
                veps[0] += 1
                o(e.scalar_tensor_tensor(out=H3[:, t, :], in0=XRES[:, t, :], scalar=col(1)[:, one], in1=NR[:, :],
                                         op0=ALU.add, op1=ALU.mult))
                inv_sqrt(e, col(2)[:, one], col(3)[:, one], col(5)[:, one], veps[0])
                e.sem_inc(s("ln"), 1)
            e.wait_ge(s("h"), 8 + 4 * GC)
            hidden_quant(0)
            down_weights(0, 1)
            hidden_integers(0)
            down_weights(1, 7)
            hidden_quant(1)
            down_weights(7, 9)
            hidden_integers(1)
            down_weights(9, GC)
            hidden_quant(2)
            hidden_integers(2)
            second_residual(0)
            hidden_quant(3)
            hidden_integers(3)
            e.wait_ge(s("x3"), 1)
            e.wait_ge(s("norm_in"), 64)
            router_rows(0)
            for t in range(1, NT):
                if t == NT - 1:
                    split(0, 0)
                second_residual(t)
                e.wait_ge(s("x3"), t + 1)
                if t == NT - 1:
                    router_evac(0)
                router_rows(t)

            for t in range(1, NT):
                router_evac(t)
            rows_lo(0)
            split(0, 1)
            e.wait_ge(s("lg_pe"), NT)
            o(e.tensor_copy(LG[:, :, :], bank[7][:, 0:32].rearrange("p (a b) -> p a b", a=NT)))
            for t in range(NT):
                ins = e.max(M8[:, t, :], LG[:, t, :])
            o(ins)
            for t in range(NT):
                ins = e.max_index(I8[:, t, :], M8[:, t, :], LG[:, t, :])
            o(ins)
            o(e.tensor_copy(I8F[:, :, :], I8[:, :, :]))
            e.tensor_tensor(E1[:, :, :], M8[:, :, 1:2], M8[:, :, 0:1], ALU.subtract).then_inc(s("top"), 1)
            for k in range(2):
                for t in range(NT):
                    ins = e.tensor_scalar(M0B[:, k, t, :], IOTA8[:, :], I8F[:, t, k:k + 1], None, ALU.is_equal)
            o(ins)
            e.tensor_tensor(MSB[:, :, :], M0B[:, 0, :, :], M0B[:, 1, :, :], ALU.add).then_inc(s("slots_m"), 1)
            split(0, 2)
            shared_tile(0)
            shared_result(0)
            e.wait_ge(s("pos_pe"), 1)
            n_e = bank[7][:, 96:104]
            o(e.memset(CTF[:, :], 0.0))
            o(e.memset(CTF[:, 0:1], float(NT)))
            o(e.memset(CTF[:, 11:12], float(NT)))
            o(e.tensor_copy(NEF[:, :], n_e))
            o(e.tensor_scalar(CTF[:, 1:9], NEF[:, :], float(P), 1.0, ALU.is_gt, ALU.add))
            for k in (2, 3):
                o(e.scalar_tensor_tensor(out=CTF[:, 1:9], in0=NEF[:, :], scalar=float(k * P), in1=CTF[:, 1:9],
                                         op0=ALU.is_gt, op1=ALU.add))
            for k in range(1, NE):
                o(e.tensor_tensor(CTF[:, 11 + k:12 + k], CTF[:, 10 + k:11 + k], CTF[:, k:k + 1], ALU.add))
            o(e.tensor_tensor(CTF[:, 31:32], CTF[:, 18:19], CTF[:, 8:9], ALU.add))
            e.tensor_copy(CNT[:, :], CTF[0:1, :]).then_inc(s("cnt"), 1)
            for t in range(NT):
                ins = e.scalar_tensor_tensor(out=AT[:, t, :], in0=CTF[:, 11:19], scalar=float(P),
                                             in1=bank[7][:, 64 + 8 * t:72 + 8 * t], op0=ALU.mult, op1=ALU.add)
            o(ins)
            for k in range(2):
                ins = e.tensor_tensor(SLM[:, k, :, :], AT[:, :, :], M0B[:, k, :, :], ALU.mult)
            o(ins)
            o(e.tensor_reduce(SLF[:, :], SLM[:, :, :, :].rearrange("p k t e -> p (k t) e"), AX.X, ALU.add))
            e.tensor_scalar(SLOT[:, :, :].rearrange("p a b -> p (a b)"), SLF[:, :], float(-BLK0 * P), None, ALU.add)\
                .then_inc(s("slots"), 1)
            shared_tile(1)
            shared_result(1)
            e.wait_ge(s("e1"), 1)
            o(e.tensor_scalar(WT[:, 2, :], WT[:, 1, :], 1.0, None, ALU.add))
            o(e.reciprocal(WT[:, 0, :], WT[:, 2, :]))
            o(e.tensor_tensor(WT[:, 1, :], WT[:, 1, :], WT[:, 0, :], ALU.mult))
            shared_tile(2)
            shared_result(2)
            shared_tile(3)
            split(1, 0)
            split(1, 1)
            shared_result(3)
            split(1, 2)

            def tile(t):
                result(t)
                hidden(t)
                rows_lo(t + 1)

            def split_all(gi):
                for m in range(3):
                    split(gi, m)
            e.wait_ge(s("cnt"), 1)
            with e.Fori(1, NE) as gi:
                n, t0 = group_of(e, gi)
                with e.Fori(0, n) as i:
                    tile(t0 + i)
                split_all(gi + 1)
            n, t0 = group_of(e, NE)
            with e.Fori(0, n) as i:
                tile(t0 + i)
            total = e.value_load(CNT[0:1, 31:32], min_val=NT + NE, max_val=MAXT)
            result(total)
            for t in range(NT):
                v = XRES[:, t, :]
                e.wait_ge(s(f"fin_in{t}"), 16 * 2)
                o(e.scalar_tensor_tensor(out=v, in0=GA[:, t, :], scalar=WT[:, 0, t:t + 1], in1=v,
                                         op0=ALU.mult, op1=ALU.add))
                e.scalar_tensor_tensor(out=v, in0=GB[:, t, :], scalar=WT[:, 1, t:t + 1], in1=v,
                                       op0=ALU.mult, op1=ALU.add).then_inc(s("fin"), 1)

        @blk.scalar
        def _(e):
            def normed(dst, t, name):
                e.activation(dst, XRES[:, t, :], ACT.Identity, bias=col(1)[:, t:t + 1], scale=col(0)[:, t:t + 1])\
                    .then_inc(s(name), 1)

            e.wait_ge(s("ctx_in"), 16)
            e.activation(CTH[:, :, :], CTX[:, :, :], ACT.Copy).then_inc(s("ct_hi"), 1)
            e.wait_ge(in_a[0], 16)
            e.activation(WVH[:, :, :], r3(RA[0][:, :], 2), ACT.Copy).then_inc(s("wv_hi"), 1)

            def v_left(t):
                e.wait_ge(s("v_pe"), 2 * t + 1)
                e.activation(V[:, t, 0:512], bank[VB[2 * t % 4]], ACT.Copy).then_inc(s("v_ev0"), 1)

            def xt_evac(t):
                for q in range(2):
                    n = 2 * t + q
                    e.wait_ge(s("xt_pe"), n + 1)
                    e.activation(XTH[:, 4 * q:4 * q + 4, t * P:t * P + P], r3(bank[2 + n % 4], 4), ACT.Copy)\
                        .then_inc(s("xt_hi"), 1)

            def w_hi(c):
                e.wait_ge(in_a[0], c * 16 + 32)
                e.activation(WQH[:, :, :].rearrange("p a b -> p (a b)"), RA[0][:, 0:STRIP], ACT.Copy)\
                    .then_inc(s("wq_hi"), 1)
            v_left(0)
            root(e, col(2), col(3))
            e.wait_ge(s("ln"), 1)
            normed(XN[0][:, :], 0, "xn")
            v_left(1)
            normed(XN[1][:, :], 1, "xn")
            v_left(2)
            v_left(3)
            for t in range(NT):
                xt_evac(t)
                if t == 0:
                    w_hi(0)
                if t + 2 < NT:
                    e.wait_ge(s("xt_pe"), 2 * (t + 1))
                    normed(XN[t % 2][:, :], t + 2, "xn")

            def absum(j, column, n):
                e.wait_ge(in_a[j], n)
                e.activation(RA[j][:, :], RA[j][:, :], ACT.Abs, accum_out=ACCW[:, column]).then_inc(free_a[j], 1)

            def close_probs(c):
                for h in range(2):
                    e.wait_ge(s("t_pe"), 2 * c - 1 + h)
                    e.activation(PTH[h][:, :], STR[h][:, 0:STRIP], ACT.Copy).then_inc(s("pt_hi"), 1)

            def close_out(c):
                for h in range(2):
                    rows = slice(HD * h, HD * h + HD)
                    e.wait_ge(s("av_pe"), 2 * c - 1 + h)
                    e.activation(OTH[rows, bass.ds(c - 1, 1), :].rearrange("p a n -> p (a n)"), bank[6 + h][rows, :],
                                 ACT.Copy).then_inc(s("ot_hi"), 1)

            def pair(c, first, last):
                e.wait_ge(s("q_pe"), c + 1)
                e.activation(QH[:, :], bank[6], ACT.Copy, scale=HD ** -0.5).then_inc(s("q_hi"), 1)
                e.wait_ge(s("k_pe"), c + 1)
                e.activation(KH[:, :], bank[7], ACT.Copy).then_inc(s("k_hi"), 1)
                if not first:
                    close_probs(c)
                if not last:
                    w_hi(c + 1)
                if not first:
                    close_out(c)
                else:
                    e.wait_ge(s("v_ev1"), NT)
                    e.wait_ge(s("v_ev0"), NT)
                e.activation(VH[:, :, :], V[:, :, bass.ds(c * P, P)], ACT.Copy).then_inc(s("vp_hi"), 1)
                for h in range(2):
                    e.wait_ge(s("nmax"), 2 * c + h + 1)
                    for i, off in HBLK:
                        ins = e.activation(PR[h][:, off:off + P * (i + 1)], STR[h][:, off:off + P * (i + 1)],
                                           ACT.Exp, bias=NM[:, h, i:i + 1], accum_out=RS[:, h, i:i + 1])
                    ins.then_inc(s("exp"), 1)
                absum(1, bass.ds(c * ABSP, 1), c * 16 + 16)
                absum(3, bass.ds(c * ABSP + 2, 1), c * 16 + 16)
            pair(0, True, False)
            with e.Fori(1, NPAIR - 1) as c:
                pair(c, False, False)
            pair(NPAIR - 1, False, True)

            def wo_hi(m):
                j = WO_SLOTS[m]
                e.wait_ge(in_a[j], 16 * (NPAIR + 2 if j == 0 else NPAIR + 1))
                if m >= 2:
                    e.wait_ge(s("y_pe"), m - 1)
                e.activation(WOH[m % 2][:, :, :], r3(RA[j][:, :], 2), ACT.Copy).then_inc(s("wo_hi"), 1)
            e.wait_ge(s("k_pe"), NPAIR)
            wo_hi(0)
            close_probs(NPAIR)
            wo_hi(1)
            close_out(NPAIR)
            wo_hi(2)
            wo_hi(3)
            absum(1, slice(NABS - 1, NABS), NPAIR * 16 + 16)

            def squares(T, J, t, acc, count):
                e.activation(J, T, ACT.Square, accum_out=acc).then_inc(s(count), 1)
            root(e, col(2), col(3))

            def rounded(j, n, use, which):
                e.wait_ge(in_b[j], use * 16 if isinstance(use, int) else use * 16)
                e.activation(RB[j][:, :], RB[j][:, :], ACT.Identity, bias=CST[:, 0:1], scale=SW[:, which:which + 1])\
                    .then_inc(s("rnd"), 1)
            e.wait_ge(s("wscale"), 1)
            rounded(0, 0, 1, 0)
            e.wait_ge(s("z"), 1)
            for t in range(2):
                e.activation(Z[:, t, :], Z[:, t, :], ACT.Identity, bias=CST[:, 0:1], scale=col(8)[:, t:t + 1])\
                    .then_inc(s("zrnd"), 1)
            rounded(1, 1, 1, 0)
            for t in range(NT):
                e.wait_ge(s("zt_pe"), t + 1)
                e.activation(XQ[:, :, t * P:t * P + P], r3(bank[4 + t].bitcast(bf16), 8), ACT.Copy)\
                    .then_inc(s("xq"), 1)

            def gate_group(c, p):
                for t in range(NT):
                    waits(e, ("g_pe", 4 * c + t + 2), ("h", 4 * c + t + 5))
                    e.activation(SG[:, t, :], bank[4 * p + t][:, 0:GW], ACT.Silu, scale=col(9)[:, t:t + 1])\
                        .then_inc(s("silu"), 1)
            e.wait_ge(s("zero"), 16 * (XT_TILES - NT))
            with e.Fori(0, GC // 2) as it:
                for j in (2, 3):
                    rounded(j, None, it + 1, 0)
                gate_group(it * 2, 0)
                for j in (0, 1):
                    rounded(j, None, it + 2, 0)
                gate_group(it * 2 + 1, 1)
            e.wait_ge(s("h"), 8 + 4 * (GC - 2) + 1)
            e.activation(JB0[:, :], HB[:, 0, 0:FB - GW], ACT.Square, accum_out=col(17)[:, 0:1])\
                .then_inc(s("h_sq0"), 1)
            gate_group(GC - 1, 0)

            def hidden_squares(t):
                if t:
                    e.wait_ge(s("h_sq"), t)
                at = slice(0, FB) if t else slice(FB - GW, FB)
                squares(HB[:, t, at], JB[:, at], t, col(10)[:, t:t + 1], "h_sq")

            def down_round(i0, i1):
                for i in range(i0, i1):
                    n = 2 * GC + i
                    rounded(n % 4, n, n // 4 + 1, 1)

            def hidden_t(t):
                for q, (k0, k1) in enumerate(HGRP):
                    e.wait_ge(s("ht_pe"), 3 * t + q + 1)
                    e.activation(HQT[t % 2][:, k0:k1, :], r3(bank[4 + q].bitcast(bf16)[:, 0:P * (k1 - k0)], k1 - k0),
                                 ACT.Copy).then_inc(s("hqt"), 1)
            def hidden_round(t):
                root(e, col(4)[:, t:t + 1], col(3)[:, t:t + 1])
                e.wait_ge(s("hz"), t + 1)
                e.activation(HB[:, t, :], HB[:, t, :], ACT.Identity, bias=CST[:, 0:1], scale=col(6)[:, t:t + 1])\
                    .then_inc(s("hrnd"), 1)

            def split(gi, t0, ms=(0, 1, 2)):
                for m in ms:
                    if t0 is not None:
                        e.wait_ge(s(("gate_pe", "up_pe", "y2_pe")[m]), t0 + (m == 2))
                    for q in range(2):
                        e.wait_ge(in_c[2 * m + q], gi * 16 + 16)
                        e.activation(WH[m][:, q * RAW:q * RAW + RAW], RC[2 * m + q][:, :], ACT.Copy)\
                            .then_inc(s("m_hi"), 1)

            def router_rows(t):
                root(e, col(2)[:, t:t + 1], col(3)[:, t:t + 1])
                e.wait_ge(s("ln"), t + 2)
                e.activation(H3[:, t, :], H3[:, t, :], ACT.Copy, scale=col(5)[:, t:t + 1]).then_inc(s("h3"), 1)
            e.wait_ge(s("h"), 8 + 4 * GC)
            hidden_squares(0)
            down_round(0, 1)
            hidden_round(0)
            down_round(1, 4)
            hidden_t(0)
            hidden_squares(1)
            down_round(4, 8)
            hidden_round(1)
            down_round(8, GC)
            hidden_squares(2)
            hidden_t(1)
            hidden_squares(3)
            hidden_round(2)
            hidden_t(2)
            hidden_round(3)
            router_rows(0)
            hidden_t(3)
            router_rows(1)
            split(0, None, (0,))
            router_rows(2)

            for t in range(NT):
                if t == 1:
                    router_rows(3)
                e.wait_ge(s("h3t_pe"), 2 * t + 1)
                if t:
                    e.wait_ge(s("lg_pe"), t)
                e.activation(H3T[:, 0:4, :], r3(bank[HB3[t % 2][0]], 4), ACT.Copy).then_inc(s("h3t"), 1)

            def rows_hi(t):
                for q in range(2):
                    e.wait_ge(s("et_pe"), t * 2 + q + 1)
                    e.activation(ETH[:, 4 * q:4 * q + 4, :], r3(bank[4 + q], 4), ACT.Copy).then_inc(s("et_hi"), 1)
            rows_hi(0)
            e.wait_ge(s("lg_pe"), NT)
            split(0, None, (1, 2))

            def result(t):
                waits(e, ("y2_pe", t + 1), ("y_st", t * 16 + 16))
                e.activation(YS[:, 0:512], bank[2], ACT.Copy).then_inc(s("ys_a"), 1)

            def hidden(t):
                e.wait_ge(s("gate_pe"), t + 1)
                e.activation(SI[:, :], bank[0], ACT.Silu).then_inc(s("esilu"), 1)
                e.wait_ge(s("ht2_pe"), t + 1)
                e.activation(HTH[:, :, :], r3(bank[6], 4), ACT.Copy).then_inc(s("ht_hi"), 1)
                rows_hi(t + 1)
            def tile(t):
                result(t)
                hidden(t)
            hidden(0)
            e.wait_ge(s("top"), 1)
            e.activation(WT[:, 1, :], E1[:, :, :].rearrange("p a b -> p (a b)"), ACT.Exp).then_inc(s("e1"), 1)
            for t in range(1, NT):
                hidden(t)
            e.sem_inc(s("ys_a"), NT)
            split(1, NT)
            e.wait_ge(s("ys_d"), NT)
            e.wait_ge(s("cnt"), 1)
            with e.Fori(1, NE) as gi:
                n, t0 = group_of(e, gi)
                with e.Fori(0, n) as i:
                    tile(t0 + i)
                split(gi + 1, t0 + n)
            n, t0 = group_of(e, NE)
            with e.Fori(0, n) as i:
                tile(t0 + i)
            total = e.value_load(CNT[0:1, 31:32], min_val=NT + NE, max_val=MAXT)
            result(total)

        @blk.tensor
        def _(e):
            e.sem_inc(s("g_pe"), 1)
            e.wait_ge(s("ct_lo"), 1)
            e.wait_ge(free_a[0], 1)
            for n in range(2 * NT):
                t, q = divmod(n, 2)
                if n >= 4:
                    e.wait_ge(s(f"v_ev{n % 2}"), (n - 4) // 2 + 1)
                three(e, bank[VB[n % 4]], [(CTH[:, k, t * P:t * P + P], CTL[:, k, t * P:t * P + P],
                                            WVH[:, k, q * 512:q * 512 + 512], WVL[:, k, q * 512:q * 512 + 512])
                                           for k in range(KL)], True, True).then_inc(s("v_pe"), 1)
            e.wait_ge(s("const"), 13)
            for t in range(NT):
                e.wait_ge(s("xn"), t + 1)
                for q in range(2):
                    n = 2 * t + q
                    if n >= 4:
                        e.wait_ge(s("xt_lo"), n - 3)
                    for k in range(4):
                        m = e.transpose(bank[2 + n % 4][:, k * P:k * P + P],
                                        XN[t % 2][:, (4 * q + k) * P:(4 * q + k + 1) * P], IDF[:, :])
                    m.then_inc(s("xt_pe"), 1)
            e.wait_ge(s("v_ev0"), NT)
            e.wait_ge(s("v_ev1"), NT)
            e.wait_ge(s("xt_lo"), 2 * NT)

            def project(c, first):
                e.wait_ge(free_a[0], c + 2)
                if not first:
                    e.wait_ge(s("ot_lo"), 2 * c - 1)
                three(e, bank[6], [(WQH[:, k, :], WQL[:, k, :], XTH[:, k, :], XTL[:, k, :]) for k in range(KD)],
                      True, True).then_inc(s("q_pe"), 1)
                three(e, bank[7], [(WQH[:, KD + k, :], WQL[:, KD + k, :], CTH[:, k, :], CTL[:, k, :])
                                   for k in range(KL)], True, True).then_inc(s("k_pe"), 1)

            def scores(c):
                e.wait_ge(s("q_lo"), c + 1)
                e.wait_ge(s("k_lo"), c + 1)
                for h in range(2):
                    rows = slice(HD * h, HD * h + HD)
                    for i, off in HBLK:
                        w = P * (i + 1)
                        q = slice(i * P, i * P + P)
                        three(e, STR[h][:, off:off + w], [(QH[rows, q], QL[rows, q], KH[rows, 0:w], KLo[rows, 0:w])],
                              True, False)
                        m = e.matmul(STR[h][:, off + i * P:off + w], IDB[:, :], MASK[:, :], start=False, stop=True)
                    m.then_inc(s("s_pe"), 1)

            def attend(c, wait_banks):
                for h in range(2):
                    e.wait_ge(s("pn"), 2 * c - 1 + h)
                    for i, off in HBLK:
                        for j in range(i + 1):
                            at = TOFF[j] + (i - j) * P
                            m = e.transpose(STR[h][:, at:at + P], PR[h][:, off + j * P:off + j * P + P], IDF[:, :])
                    m.then_inc(s("t_pe"), 1)
                if wait_banks:
                    e.wait_ge(s("q_lo"), c + 1)
                    e.wait_ge(s("k_lo"), c + 1)
                e.wait_ge(s("vp_lo"), c)
                def part(h, V1, P1, first, last):
                    for j in range(NT):
                        off, w = TOFF[j], TOK - j * P
                        m = e.matmul(bank[6 + h][:, j * P:TOK], V1[:, j, :], P1[h][:, off:off + w],
                                     start=first and j == 0, stop=last and j == NT - 1)
                    return m
                for h in range(2):
                    e.wait_ge(s("pt_hi"), 2 * c - 1 + h)
                    part(h, VH, PTH, True, False)
                    part(h, VL, PTH, False, False)
                for h in range(2):
                    e.wait_ge(s("pt_lo"), 2 * c - 1 + h)
                    part(h, VH, PTL, False, True).then_inc(s("av_pe"), 1)
            project(0, True)
            scores(0)
            with e.Fori(1, NPAIR) as c:
                project(c, False)
                attend(c, True)
                scores(c)
            attend(NPAIR, False)
            steps = [(m, t) for m in range(2) for t in range(NT)] + \
                [(2, 0), (2, 1), (3, 0), (2, 2), (3, 1), (2, 3), (3, 2), (3, 3)]
            for m, t in steps:
                if t == 0:
                    e.wait_ge(s("wo_lo"), m + 1)
                if m == 0 and t == NT - 1:
                    e.wait_ge(s("ot_lo"), 2 * NPAIR + 1)
                for q in range(2):
                    cs = slice(q * 512, q * 512 + 512)
                    ins = three(e, bank[2 * t + q],
                                [(OTH[:, k, t * P:t * P + P], OTL[:, k, t * P:t * P + P],
                                  WOH[m % 2][:, k % 2, cs], WOL[m % 2][:, k % 2, cs]) for k in (2 * m, 2 * m + 1)],
                                m == 0, m == 3)
                if m == 3:
                    ins.then_inc(s("y_tile"), 1)
                elif m < 2 and t == NT - 1:
                    ins.then_inc(s("y_pe"), 1)
            e.wait_ge(s("wsum"), 1)
            e.wait_ge(s("x2"), 1)
            e.matmul(bank[0][:, 0:2], ONEF[:, :], WS[:, :], start=True, stop=True).then_inc(s("wsum_pe"), 1)

            for t in range(NT):
                e.wait_ge(s("zq"), t + 1)
                for k in range(KD):
                    m = e.transpose(bank[4 + t].bitcast(bf16)[:, k * P:k * P + P], ZQ[t % 2][:, k * P:k * P + P],
                                    IDB[:, :])
                m.then_inc(s("zt_pe"), 1)
            e.wait_ge(s("xq"), NT)
            e.wait_ge(s("z"), 1)

            def gate_group(c, p):
                e.wait_ge(s("tern"), c * 2 + 2)
                for t in range(NT):
                    e.wait_ge(s("h"), 4 * c + t + 1)
                    for k in range(KD):
                        m = e.matmul(bank[4 * p + t], XQ[:, k, t * P:t * P + P], TG[p][:, k, :],
                                     start=k == 0, stop=k == KD - 1)
                    m.then_inc(s("g_pe"), 1)
            with e.Fori(0, GC // 2) as it:
                gate_group(it * 2, 0)
                gate_group(it * 2 + 1, 1)
            gate_group(GC - 1, 0)
            e.wait_ge(s("h"), 8 + 4 * GC)

            def hidden_t(t):
                e.wait_ge(s("hq"), t + 1)
                for q, (k0, k1) in enumerate(HGRP):
                    if t:
                        e.wait_ge(s("hqt"), 3 * (t - 1) + q + 1)
                    for k in range(k0, k1):
                        m = e.transpose(bank[4 + q].bitcast(bf16)[:, (k - k0) * P:(k - k0 + 1) * P],
                                        HQ[:, k * P:k * P + P], IDB[:, :])
                    m.then_inc(s("ht_pe"), 1)

            hidden_t(0)
            for t in range(NT):
                e.wait_ge(s("hqt"), 3 * t + 3)
                if t >= 2:
                    e.wait_ge(s("x3"), t - 1)
                for q in range(2):
                    for k in range(KB):
                        if t == 0 and q == 0 and k % 2 == 0:
                            e.wait_ge(s("tern"), 2 * GC + k // 2 + 1)
                        m = e.matmul(bank[2 * (t % 2) + q], HQT[t % 2][:, k, :], TD[:, k, q * 512:q * 512 + 512],
                                     start=k == 0, stop=k == KB - 1)
                    m.then_inc(s("d_pe"), 1)
                    if q == 0 and t + 1 < NT:
                        hidden_t(t + 1)

            def router_t(t):
                e.wait_ge(s("h3"), t + 1)
                if t == 0:
                    e.wait_ge(s("x3"), NT - 1)
                if t >= 2:
                    e.wait_ge(s("h3t"), 2 * (t - 1))
                for q in range(2):
                    for k in range(4):
                        m = e.transpose(bank[HB3[t % 2][q]][:, k * P:k * P + P],
                                        H3[:, t, (4 * q + k) * P:(4 * q + k + 1) * P], IDF[:, :])
                    m.then_inc(s("h3t_pe"), 1)

            def logits(t):
                e.wait_ge(s("h3t"), 2 * t + 2)
                for k in range(KD):
                    m = e.matmul(bank[7][:, 8 * t:8 * t + 8], H3T[:, k, :], WR[:, k, :],
                                 start=k == 0, stop=k == KD - 1)
                m.then_inc(s("lg_pe"), 1)

            def ranks():
                e.wait_ge(s("slots_m"), 1)
                for t in range(NT):
                    for u in range(t + 1):
                        e.matmul(bank[7][:, 64 + 8 * t:72 + 8 * t], (TRI if u == t else ONEB)[:, :], MSB[:, u, :],
                                 start=u == 0, stop=u == t)
                for t in range(NT):
                    m = e.matmul(bank[7][:, 96:104], ONEB[:, :], MSB[:, t, :], start=t == 0, stop=t == NT - 1)
                m.then_inc(s("pos_pe"), 1)

            def rows_t(t, q, rows):
                if q == 0 and rows is None:
                    e.wait_ge(s("e_in"), t * 16 + 16)
                for k in range(4):
                    cs = slice((4 * q + k) * P, (4 * q + k + 1) * P)
                    m = e.transpose(bank[4 + q][:, k * P:k * P + P], XG[:, cs] if rows is None else rows[:, cs],
                                    IDF[:, :])
                m.then_inc(s("et_pe"), 1)
            router_t(0)
            for t in range(NT):
                if t + 1 < NT:
                    router_t(t + 1)
                logits(t)

            def tile(t, gi, rows=None):
                waits(e, ("et_hi", t * 2 + 2), (free_c[0], gi + 1))
                for m in range(2):
                    for q in range(2):
                        if m or q:
                            waits(e, (free_c[2 * m + q], gi + 1))
                        highs(e, bank[m], [(ETH[:, k, :], WH[m][:, k * FE:k * FE + FE], WL[m][:, k * FE:k * FE + FE])
                                           for k in range(4 * q, 4 * q + 4)], q == 0)
                    e.wait_ge(s("et_lo"), t * 2 + 2)
                    lows(e, bank[m], [(ETL[:, k, :], WH[m][:, k * FE:k * FE + FE]) for k in range(KD)])\
                        .then_inc(s(("gate_pe", "up_pe")[m]), 1)
                rows_t(t + 1, 0, rows)
                e.wait_ge(s("eh"), t + 1)
                for k in range(KE):
                    m = e.transpose(bank[6][:, k * P:k * P + P], HE[:, k * P:k * P + P], IDF[:, :])
                m.then_inc(s("ht2_pe"), 1)
                rows_t(t + 1, 1, rows)
                left = [("ys_a", t + 1), ("ys_d", t + 1)] if not isinstance(gi, int) or gi else [("ys_d", t)]
                waits(e, ("ht_hi", t + 1), *left, (free_c[4], gi + 1), (free_c[5], gi + 1))

                def at(k, q):
                    return slice(k * DM + q * 512, k * DM + q * 512 + 512)
                for q in range(2):
                    highs(e, bank[2 + q], [(HTH[:, k, :], WH[2][:, at(k, q)], WL[2][:, at(k, q)])
                                           for k in range(KE)])
                e.wait_ge(s("ht_lo"), t + 1)
                for q in range(2):
                    m = lows(e, bank[2 + q], [(HTL[:, k, :], WH[2][:, at(k, q)]) for k in range(KE)])
                m.then_inc(s("y2_pe"), 1)
            rows_t(0, 0, H3[:, 0, :])
            rows_t(0, 1, H3[:, 0, :])
            e.sem_inc(s("y2_pe"), 1)
            for t in range(NT):
                tile(t, 0, H3[:, t + 1, :] if t + 1 < NT else None)
                if t == 0:
                    ranks()
            e.wait_ge(s("cnt"), 1)
            with e.Fori(1, NE) as gi:
                n, t0 = group_of(e, gi)
                with e.Fori(0, n) as i:
                    tile(t0 + i, gi)
            n, t0 = group_of(e, NE)
            with e.Fori(0, n) as i:
                tile(t0 + i, NE)


def kernel(**inputs):
    import numpy as np
    import concourse.bacc as bacc
    from concourse.bass_utils import run_bass_kernel_spmd

    g = {k: np.asarray(v) for k, v in inputs.items()}

    def chunks(wt, n_out):
        k, o = wt.shape
        return wt.reshape(k // P, P, o // n_out, n_out).transpose(2, 1, 0, 3)

    def halves(a):
        n, p, w = a.shape
        return a.reshape(n, p, w // RAW, RAW).transpose(0, 2, 1, 3).reshape(-1, p, RAW)

    wkv = g["L0_xattn_Wkv_expand"]
    wq_c = chunks(g["L0_xattn_Wq"].T, P).reshape(NPAIR, P, KD * P)
    wk_c = chunks(wkv[:DM].T, P).reshape(NPAIR, P, KL * P)
    wg = g["L0_attn_w_gate"]
    gate_up = np.concatenate([wg[:FB].T.reshape(DM, GC, 1, GW), wg[FB:].T.reshape(DM, GC, 1, GW)], axis=2)
    gate_c = halves(chunks(gate_up.reshape(DM, 2 * FB), 2 * GW).reshape(GC, P, KD * 2 * GW))
    down_c = g["L0_attn_w_down"].T.reshape(GC, 2, P, DM).transpose(0, 2, 1, 3).reshape(GC, P, RAW)

    def expert(wgate, wup, wdown):
        def rows(a, k):
            return a.reshape(k, P, -1).transpose(1, 0, 2).reshape(1, P, 2 * RAW)
        return [halves(rows(wgate, KD)), halves(rows(wup, KD)), halves(rows(wdown, KE))]

    moe = expert(g["L0_ffn_sw_gate"], g["L0_ffn_sw_up"], g["L0_ffn_sw_down"])
    for k in range(NE):
        moe += expert(g["L0_ffn_w_gate"][k], g["L0_ffn_w_up"][k], g["L0_ffn_w_down"][k])
    arrays = {
        "x": g["x"][0],
        "ctxT": g["ctx_512"][0, :TOK].T.reshape(KL, P, TOK).transpose(1, 0, 2),
        "wv": wkv[DM:].T.reshape(KL, P, DM).transpose(1, 0, 2).reshape(P, RAW),
        "wqk": np.concatenate([wq_c, wk_c], axis=2),
        "wo": g["L0_xattn_Wout"].T.reshape(4, 2, P, DM).transpose(0, 2, 1, 3).reshape(4, P, RAW),
        "wbit": np.concatenate([gate_c, down_c], axis=0),
        "n_gate": g["L0_attn_norm_gate"], "n_down": g["L0_attn_norm_down"], "n_rms": g["L0_ffn_rms_weight"],
        "wrt": g["L0_ffn_router_w"].reshape(KD, P, NE).transpose(1, 0, 2),
        "wmoe": np.concatenate(moe, axis=0),
    }
    arrays = {k: np.ascontiguousarray(v) for k, v in arrays.items()}
    nc = bacc.Bacc("TRN2", target_bir_lowering=False, num_devices=1)
    args = [nc.dram_tensor(n, v.shape, mybir.dt.from_np(v.dtype), kind="ExternalInput").ap()
            for n, v in arrays.items()]
    out = nc.dram_tensor("out", (TOK, DM), f32, kind="ExternalOutput").ap()
    rows = nc.dram_tensor("rows", (DRAM_TILES * P, DM), f32, kind="Internal").ap()
    program(nc, *args, out, rows)
    r = run_bass_kernel_spmd(nc, [arrays], core_ids=[0])
    return r.results[0]["out"].reshape(1, TOK, DM)
```
